# Optimizing a Trainium2 kernel written in Bass

```python
import numpy as np
import jax
import jax.numpy as jnp

def _softmax(x, axis=-1):
    return jax.nn.softmax(x, axis=axis)

def _gelu(x):
    return jax.nn.gelu(x, approximate=True)

def _silu(x):
    return jax.nn.silu(x)

def _sigmoid(x):
    return jax.nn.sigmoid(x)

def _layernorm(x, axis=-1, eps=1e-05):
    m = jnp.mean(x, axis=axis, keepdims=True)
    v = jnp.var(x, axis=axis, keepdims=True)
    return (x - m) / jnp.sqrt(v + eps)

def _scatter_add(tgt, idx, src, axis=0):
    return tgt.at[idx].add(src)

def _segment_sum(src, seg, n):
    return jax.ops.segment_sum(src, seg, n)
kernel_name = 'mk_gnn_preln_d1_gnn_r32_3cd6ac'

def setup_inputs(seed: int=0):
    np.random.seed(seed)
    _w = jnp.asarray

    def _rec_inputs():
        import jax
        import jax.numpy as jnp
        _gk = jax.random.key(seed)
        x = -0.0006008 + 1.001 * jax.random.normal(jax.random.fold_in(_gk, 1), (50000, 512), jnp.float32)
        src = jax.random.randint(jax.random.fold_in(_gk, 2), (25000,), 0, 50000, jnp.int32)
        dst = jnp.minimum((50000 * jax.random.uniform(jax.random.fold_in(_gk, 3), (25000,)) ** 2.0).astype(jnp.int32), 49999)
        _o = jnp.argsort(dst, stable=True)
        src = src[_o]
        dst = dst[_o]
        edge_attr_20 = jax.random.uniform(jax.random.fold_in(_gk, 12), (25000, 20), jnp.float32, 0.0, 0.999999)
        edge_attr_3 = -0.0005747 + 0.998114 * jax.random.normal(jax.random.fold_in(_gk, 13), (25000, 3), jnp.float32)
        edge_weight = jax.random.uniform(jax.random.fold_in(_gk, 14), (25000,), jnp.float32, 0.0, 0.999973)
        return (x, src, dst, edge_attr_20, edge_attr_3, edge_weight)
    x, src, dst, edge_attr_20, edge_attr_3, edge_weight = _rec_inputs()

    def _L0_gnn_setup():
        import jax, jax.numpy as jnp
        import numpy as np
        N_ATOMS = 5000
        N_EDGES = 50000
        C = 128
        F = 128
        N_RBF = 20
        LOG2 = float(np.log(2.0))
        Y0 = float(1.0 / np.sqrt(4.0 * np.pi))
        Y1_SCALE = float(np.sqrt(3.0 / (4.0 * np.pi)))

        def shifted_softplus(x):
            return jax.nn.softplus(x) - LOG2

        def _forward(x, idx_i, idx_j, f_ij, rcut_ij, r_ij, W_in2f_s, W_in2f_v, Wf1, bf1, Wf2, bf2, W1_s, W1_v, W2_s, W2_v):
            n = x.shape[0]
            e = r_ij.shape[0]
            xs = x[:, :C] @ (W_in2f_s / np.sqrt(C))
            xv = jnp.einsum('nci,cf->nfi', x[:, C:].reshape(n, C, 3), W_in2f_v) / np.sqrt(C)
            sj = xs[idx_j]
            vj = xv[idx_j]
            u = r_ij / jnp.linalg.norm(r_ij, axis=-1, keepdims=True)
            Yv = Y1_SCALE * u
            o0a = sj * Y0
            o0b = jnp.einsum('efi,ei->ef', vj, Yv) / np.sqrt(3.0)
            s2 = jnp.stack([o0a, o0b], axis=-1).reshape(e, 2 * F)
            ova = sj[:, :, None] * Yv[:, None, :]
            ovb = vj * Y0
            v2 = jnp.stack([ova, ovb], axis=2)
            w1 = jnp.cross(vj, Yv[:, None, :]) / np.sqrt(2.0)
            ax, ay, az = (vj[..., 0], vj[..., 1], vj[..., 2])
            bx, by, bz = (Yv[:, None, 0], Yv[:, None, 1], Yv[:, None, 2])
            t = jnp.stack([(ax * by + ay * bx) / np.sqrt(2.0), (ay * bz + az * by) / np.sqrt(2.0), (2.0 * az * bz - ax * bx - ay * by) / np.sqrt(6.0), (az * bx + ax * bz) / np.sqrt(2.0), (ax * bx - ay * by) / np.sqrt(2.0)], axis=-1)
            h = shifted_softplus(f_ij @ Wf1 + bf1)
            W = (h @ Wf2 + bf2) * rcut_ij[:, None]
            m_s = s2 * W[:, :2 * F]
            m_v = (v2.reshape(e, 2 * F, 3) * W[:, 2 * F:4 * F, None]).reshape(e, 6 * F)
            m_w = (w1 * W[:, 4 * F:5 * F, None]).reshape(e, 3 * F)
            m_t = (t * W[:, 5 * F:6 * F, None]).reshape(e, 5 * F)
            x_ij = jnp.concatenate([m_s, m_v, m_w, m_t], axis=1)
            agg = jax.ops.segment_sum(x_ij, idx_i, num_segments=n)
            S = agg[:, :2 * F] @ (W1_s / np.sqrt(2 * F))
            V = jnp.einsum('nmi,mc->nci', agg[:, 2 * F:8 * F].reshape(n, 2 * F, 3), W1_v) / np.sqrt(2 * F)
            S = shifted_softplus(S)
            S = S @ (W2_s / np.sqrt(C))
            V = jnp.einsum('nci,cd->ndi', V, W2_v) / np.sqrt(C)
            return jnp.concatenate([S, V.reshape(n, 3 * C)], axis=1)
        key = jax.random.key(seed)
        ks = jax.random.split(key, 16)
        f32 = jnp.float32
        x = jax.random.normal(ks[0], (N_ATOMS, 4 * C), f32)
        idx_i = jnp.sort(jax.random.randint(ks[1], (N_EDGES,), 0, N_ATOMS))
        idx_j = jax.random.randint(ks[2], (N_EDGES,), 0, N_ATOMS)
        f_ij = jax.random.uniform(ks[3], (N_EDGES, N_RBF), f32)
        rcut_ij = jax.random.uniform(ks[4], (N_EDGES,), f32)
        r_ij = jax.random.normal(ks[5], (N_EDGES, 3), f32)
        W_in2f_s = jax.random.normal(ks[6], (C, F), f32)
        W_in2f_v = jax.random.normal(ks[7], (C, F), f32)
        Wf1 = jax.random.normal(ks[8], (N_RBF, F), f32) / np.sqrt(N_RBF)
        bf1 = 0.1 * jax.random.normal(ks[9], (F,), f32)
        Wf2 = jax.random.normal(ks[10], (F, 6 * F), f32) / np.sqrt(F)
        bf2 = 0.1 * jax.random.normal(ks[11], (6 * F,), f32)
        W1_s = jax.random.normal(ks[12], (2 * F, C), f32)
        W1_v = jax.random.normal(ks[13], (2 * F, C), f32)
        W2_s = jax.random.normal(ks[14], (C, C), f32)
        W2_v = jax.random.normal(ks[15], (C, C), f32)
        return dict(x=x, idx_i=idx_i, idx_j=idx_j, f_ij=f_ij, rcut_ij=rcut_ij, r_ij=r_ij, W_in2f_s=W_in2f_s, W_in2f_v=W_in2f_v, Wf1=Wf1, bf1=bf1, Wf2=Wf2, bf2=bf2, W1_s=W1_s, W1_v=W1_v, W2_s=W2_s, W2_v=W2_v)
    _L0_gnn_all = _L0_gnn_setup()
    _L0_gnn_in = {k: v for k, v in _L0_gnn_all.items() if k in ('W_in2f_s', 'W_in2f_v', 'Wf1', 'bf1', 'Wf2', 'bf2', 'W1_s', 'W1_v', 'W2_s', 'W2_v')}
    del _L0_gnn_all
    return {'x': x, 'src': src, 'dst': dst, 'edge_attr_20': edge_attr_20, 'edge_attr_3': edge_attr_3, 'edge_weight': edge_weight, 'L0_gnn_W_in2f_s': _L0_gnn_in['W_in2f_s'], 'L0_gnn_W_in2f_v': _L0_gnn_in['W_in2f_v'], 'L0_gnn_Wf1': _L0_gnn_in['Wf1'], 'L0_gnn_bf1': _L0_gnn_in['bf1'], 'L0_gnn_Wf2': _L0_gnn_in['Wf2'], 'L0_gnn_bf2': _L0_gnn_in['bf2'], 'L0_gnn_W1_s': _L0_gnn_in['W1_s'], 'L0_gnn_W1_v': _L0_gnn_in['W1_v'], 'L0_gnn_W2_s': _L0_gnn_in['W2_s'], 'L0_gnn_W2_v': _L0_gnn_in['W2_v']}

def reference(x, src, dst, edge_attr_20, edge_attr_3, edge_weight, L0_gnn_W_in2f_s, L0_gnn_W_in2f_v, L0_gnn_Wf1, L0_gnn_bf1, L0_gnn_Wf2, L0_gnn_bf2, L0_gnn_W1_s, L0_gnn_W1_v, L0_gnn_W2_s, L0_gnn_W2_v):
    import jax
    import jax.numpy as jnp

    def _L0_gnn_ref(x, idx_i, idx_j, f_ij, rcut_ij, r_ij, W_in2f_s, W_in2f_v, Wf1, bf1, Wf2, bf2, W1_s, W1_v, W2_s, W2_v):
        import jax, jax.numpy as jnp
        import numpy as np
        N_ATOMS = 5000
        N_EDGES = 50000
        C = 128
        F = 128
        N_RBF = 20
        LOG2 = float(np.log(2.0))
        Y0 = float(1.0 / np.sqrt(4.0 * np.pi))
        Y1_SCALE = float(np.sqrt(3.0 / (4.0 * np.pi)))

        def shifted_softplus(x):
            return jax.nn.softplus(x) - LOG2

        def _forward(x, idx_i, idx_j, f_ij, rcut_ij, r_ij, W_in2f_s, W_in2f_v, Wf1, bf1, Wf2, bf2, W1_s, W1_v, W2_s, W2_v):
            n = x.shape[0]
            e = r_ij.shape[0]
            xs = x[:, :C] @ (W_in2f_s / np.sqrt(C))
            xv = jnp.einsum('nci,cf->nfi', x[:, C:].reshape(n, C, 3), W_in2f_v) / np.sqrt(C)
            sj = xs[idx_j]
            vj = xv[idx_j]
            u = r_ij / jnp.linalg.norm(r_ij, axis=-1, keepdims=True)
            Yv = Y1_SCALE * u
            o0a = sj * Y0
            o0b = jnp.einsum('efi,ei->ef', vj, Yv) / np.sqrt(3.0)
            s2 = jnp.stack([o0a, o0b], axis=-1).reshape(e, 2 * F)
            ova = sj[:, :, None] * Yv[:, None, :]
            ovb = vj * Y0
            v2 = jnp.stack([ova, ovb], axis=2)
            w1 = jnp.cross(vj, Yv[:, None, :]) / np.sqrt(2.0)
            ax, ay, az = (vj[..., 0], vj[..., 1], vj[..., 2])
            bx, by, bz = (Yv[:, None, 0], Yv[:, None, 1], Yv[:, None, 2])
            t = jnp.stack([(ax * by + ay * bx) / np.sqrt(2.0), (ay * bz + az * by) / np.sqrt(2.0), (2.0 * az * bz - ax * bx - ay * by) / np.sqrt(6.0), (az * bx + ax * bz) / np.sqrt(2.0), (ax * bx - ay * by) / np.sqrt(2.0)], axis=-1)
            h = shifted_softplus(f_ij @ Wf1 + bf1)
            W = (h @ Wf2 + bf2) * rcut_ij[:, None]
            m_s = s2 * W[:, :2 * F]
            m_v = (v2.reshape(e, 2 * F, 3) * W[:, 2 * F:4 * F, None]).reshape(e, 6 * F)
            m_w = (w1 * W[:, 4 * F:5 * F, None]).reshape(e, 3 * F)
            m_t = (t * W[:, 5 * F:6 * F, None]).reshape(e, 5 * F)
            x_ij = jnp.concatenate([m_s, m_v, m_w, m_t], axis=1)
            agg = jax.ops.segment_sum(x_ij, idx_i, num_segments=n)
            S = agg[:, :2 * F] @ (W1_s / np.sqrt(2 * F))
            V = jnp.einsum('nmi,mc->nci', agg[:, 2 * F:8 * F].reshape(n, 2 * F, 3), W1_v) / np.sqrt(2 * F)
            S = shifted_softplus(S)
            S = S @ (W2_s / np.sqrt(C))
            V = jnp.einsum('nci,cd->ndi', V, W2_v) / np.sqrt(C)
            return jnp.concatenate([S, V.reshape(n, 3 * C)], axis=1)
        return _forward(x, idx_i, idx_j, f_ij, rcut_ij, r_ij, W_in2f_s, W_in2f_v, Wf1, bf1, Wf2, bf2, W1_s, W1_v, W2_s, W2_v)
    h = jnp.maximum(_layernorm(x, axis=-1), 0.0)
    x = x + _L0_gnn_ref(h, src, dst, edge_attr_20, edge_weight, edge_attr_3, L0_gnn_W_in2f_s, L0_gnn_W_in2f_v, L0_gnn_Wf1, L0_gnn_bf1, L0_gnn_Wf2, L0_gnn_bf2, L0_gnn_W1_s, L0_gnn_W1_v, L0_gnn_W2_s, L0_gnn_W2_v)
    return x

_drawn_inputs = setup_inputs


def setup_inputs(seed=0):
    import zlib

    import numpy as np

    out = dict(_drawn_inputs(seed))
    spreads = {}
    factors = {'edge_attr_20': 5.069,
     'edge_attr_3': 3.642,
     'edge_weight': 4.78,
     'L0_gnn_W_in2f_s': 3.67,
     'L0_gnn_W_in2f_v': 3.195,
     'L0_gnn_bf1': 8.0,
     'L0_gnn_bf2': 7.645,
     'L0_gnn_W1_s': 8.0,
     'L0_gnn_W2_s': 7.87}
    for name, (base, spread) in spreads.items():
        noise = np.random.default_rng([zlib.crc32(name.encode()), seed]).standard_normal(out[name].shape)
        drawn = base * np.exp(spread * noise) if base else spread * noise
        out[name] = jnp.asarray(drawn.astype(out[name].dtype))
    for name, factor in factors.items():
        out[name] = (out[name] * factor).astype(out[name].dtype)
    return out
```

```python
import math
from contextlib import ExitStack

import concourse.bass as bass
from concourse import mybir

F32 = mybir.dt.float32
I32 = mybir.dt.int32
BF16 = mybir.dt.bfloat16
ALU = mybir.AluOpType
ACT = mybir.ActivationFunctionType

P = 128
N_NODES = 50000
N_EDGES = 25000
D = 512
C = 128
N_RBF = 20
EPS = 1e-5
LOG2 = math.log(2.0)
Y0 = 1.0 / math.sqrt(4.0 * math.pi)
Y1_SCALE = math.sqrt(3.0 / (4.0 * math.pi))

RANK_TILES = -(-N_EDGES // P)
CHUNK = 7
N_CHUNKS = RANK_TILES // CHUNK
UNROLL = 4
LAG = 2
DIGIT = 256
PAD_KEY = (N_NODES // DIGIT + 1) * DIGIT - 1
BF_SLOTS = 4
ATTR = 4 + N_RBF
REC = 32
W_NODE, W_SOURCE, W_WEIGHT, W_VEC, W_RBF = 0, 1, 2, 3, 6

GROUP = 4
REAL = P - 1
N_GROUPS = -(-N_EDGES // (GROUP * REAL))
SORTED = RANK_TILES * P
PAD_ROWS = 11
N_ROWS = 1 + SORTED + PAD_ROWS * P
SKIP = 65536.0
SLOTS = 4
assert RANK_TILES % CHUNK == 0 and N_CHUNKS % UNROLL == 0 and N_GROUPS % SLOTS == 2
assert N_ROWS > GROUP * REAL * (N_GROUPS + 2) + 1

COPY_CHUNKS = 25


def at_least(eng, sem, value):
    if not (isinstance(value, int) and value <= 0):
        eng.wait_ge(sem, value)


def wait_apart(eng, sem, value, passed):
    eng.wait_ge(sem, value)
    eng.sem_inc(passed, 1)


def gnn_kernel(nc, x, src_cols, src_rows, dst_cols, attrs, w_in_s, w_in_v, wf1, bf1, wf2, bf2,
               w1_s, w1_v, w2_s, w2_v, out):
    table = nc.dram_tensor("records_by_node", [N_ROWS, REC], F32, kind="Internal").ap()

    ctx = ExitStack()
    with ctx:
        def sb(name, shape, dt=F32):
            return ctx.enter_context(nc.sbuf_tensor(name, shape, dt))

        def sem(name):
            return ctx.enter_context(nc.semaphore(name))

        ident = sb("ident", [P, P])
        ones_m = sb("ones_m", [P, P])
        after = sb("after", [P, P])
        before = sb("before", [P, P])
        iota_f = sb("iota_f", [P, DIGIT])
        iota_b = sb("iota_b", [P, DIGIT], BF16)
        iota_p = sb("iota_p", [P, 2])
        zeros_b = sb("zeros_b", [P, DIGIT], BF16)
        ones_f = sb("ones_f", [P, DIGIT])

        prod_room = sb("prod_room", [P, 2 * 6 * GROUP * P])
        y_room = sb("y_room", [P, 2 * GROUP * D])
        prod = prod_room[:].rearrange("p (s n e) -> p s n e", s=2, n=6)
        y = y_room[:].rearrange("p (s g d) -> p s g d", s=2, g=GROUP)

        def part(room, start, *dims):
            flat = room[:, start:start + math.prod(dims)]
            if len(dims) == 1:
                return flat
            if len(dims) == 2:
                return flat.rearrange("p (a b) -> p a b", a=dims[0])
            return flat.rearrange("p (a b c) -> p a b c", a=dims[0], b=dims[1])

        onehot_t = part(prod_room, 0, 2, 2, CHUNK * P)
        keyrow = part(prod_room, 4 * CHUNK * P, 2, CHUNK * P).bitcast(I32)
        junk_same = part(prod_room, 6 * CHUNK * P, 2, P)
        count, upto, base = (part(y_room, n * 2 * DIGIT, 2, DIGIT) for n in range(3))
        counts_sb = part(y_room, 6 * DIGIT, 2, 2, DIGIT)
        junk_look = part(y_room, 10 * DIGIT, 2, DIGIT)
        hirow = part(y_room, 12 * DIGIT, CHUNK * P).bitcast(I32)
        assert 6 * CHUNK * P + 2 * P <= 2 * 6 * GROUP * P and 12 * DIGIT + CHUNK * P <= 2 * GROUP * D

        key_i = sb("key_i", [P, RANK_TILES], I32)
        dst_i = sb("dst_i", [P, RANK_TILES], I32)
        digit_i = sb("digit_i", [P, 2, RANK_TILES], I32)
        digits = sb("digits", [P, 3, RANK_TILES])
        dig = sb("dig", [P, 2, 3, CHUNK])
        onehot = sb("onehot", [P, BF_SLOTS, 2, DIGIT], BF16)
        row_total = sb("row_total", [P, 2])
        row_base = sb("row_base", [P, 2])
        looked = sb("looked", [P, 2, CHUNK])
        same = sb("same", [P, 2, CHUNK])
        place = sb("place", [P, CHUNK])
        place_i = sb("place_i", [P, 2, CHUNK], I32)
        recs = sb("recs", [P, 2, CHUNK, REC])
        padrec = sb("padrec", [P, PAD_ROWS, REC])

        wraw = sb("wraw", [P, 8, C])
        wf2_raw = sb("wf2_raw", [P, 4 * C])
        w_t = sb("w_t", [P, 2, C])
        wf1_sb = sb("wf1_sb", [N_RBF, C])
        bf1_sb = sb("bf1_sb", [P, 1])
        bf2_sb = sb("bf2_sb", [P, 4])
        wf2_sb = sb("wf2_sb", [P, 4, C])
        w_a, w_b, m_a, m_b, u_c, u_d, w2_sb = (
            sb(n, [P, C]) for n in ("w_a", "w_b", "m_a", "m_b", "u_c", "u_d", "w2_sb"))

        rec = sb("rec", [P, SLOTS, GROUP, REC + 1])
        scat_i = sb("scat_i", [P, SLOTS, GROUP], I32)
        xg = sb("xg", [P, SLOTS, GROUP, D])
        xs = sb("xs", [P, SLOTS, GROUP, D])
        stats = sb("stats", [P, GROUP, 6])
        mv = sb("mv", [P, GROUP, 2])
        sq = sb("sq", [P, GROUP, 3])
        sq_sum = sb("sq_sum", [P, GROUP])
        idx_f = sb("idx_f", [P, 3, GROUP])
        var = sb("var", [P, 8])
        rsq = sb("rsq", [P, 2, 8])
        newt = sb("newt", [P, 4, 8])
        scale = sb("scale", [P, 2, GROUP])
        unit = sb("unit", [P, SLOTS, GROUP, 3])
        gsum = sb("gsum", [P, 2, 3, GROUP, C])
        sel = sb("sel", [P, 2, GROUP, P])
        ft_sb = sb("ft_sb", [N_RBF, GROUP * P])
        fa = sb("fa", [P, 3, GROUP * P])
        fr = sb("fr", [P, GROUP * P])
        sp_t = sb("sp_t", [P, GROUP * P])
        sp_m = sb("sp_m", [P, GROUP * P])
        h_t = sb("h_t", [P, 5, GROUP * P])
        w_sb = sb("w_sb", [P, 4, GROUP * P])
        zq = sb("zq", [P, 2, C])
        s_sb = sb("s_sb", [P, GROUP, C])
        ba = sb("ba", [P, 3, GROUP * P])
        br = sb("br", [P, GROUP * P])
        ssp_t = sb("ssp_t", [P, GROUP * P])

        psum = [ctx.enter_context(nc.psum_tensor(f"bank{i}", [P, 512], F32)) for i in range(8)]
        FB = psum[0:4]
        b_sq, b_z, b_seg, b_s = psum[4:8]
        counts_ps, off_ps, look_ps = psum[0], psum[1], psum[2:4]

        S = {}
        for n in """keys_in iotas consts digits_made dig_made onehots_free onehots_made counts_read
                    totals_made offsets_made base_made counts_moved onehot_t_made looked_up look_free
                    same_made hist_step place_summed places_made pads_made pads_out
                    weights_in weights_t weights_tc weights_u weights_made copied
                    idx_made squares rsq_made newton scale_made unit_made
                    stats_made mv_made var_made h_made g_part pre_made
                    keyb_ready ft_ready h1_ready t_ready j_ready w_ready sq_ready z_ready seg_ready st_ready s2_ready
                    ft_copied h1_read f_exp f_ln t_copied w_copied sq_copied s_copied st_read b_exp b_ln
                    sel_made sel_done sp_done prod_done y_made v_added ssp_done s_added zeroed pool_passed dve_passed carried carry_start f_abs b_abs ys_made hirow_made""".split():
            S[n] = sem(n)
        chunk_keys = [sem(f"chunk_keys{h}") for h in range(2)]
        chunk_recs = [sem(f"chunk_recs{h}") for h in range(2)]
        chunk_out = [sem(f"chunk_out{h}") for h in range(2)]
        rec_in = [sem(f"rec_in{k}") for k in range(SLOTS)]
        xg_in = [sem(f"xg_in{k}") for k in range(SLOTS)]
        xs_in = [sem(f"xs_in{k}") for k in range(SLOTS)]
        rows_out = [sem(f"rows_out{k}") for k in range(SLOTS)]
        HALF = N_CHUNKS // 2
        N_LOOPS = N_GROUPS // SLOTS

        def steps(eng, step, first):
            for s in range(first, SLOTS):
                step(s, s // SLOTS, s % SLOTS)
            with eng.Fori(1, N_LOOPS) as i:
                for k in range(SLOTS):
                    step(SLOTS * i + k, i, k)
            for s in range(SLOTS * N_LOOPS, N_GROUPS):
                step(s, N_LOOPS, s % SLOTS)

        def loads(i, k, ahead, per):
            return per * 16 * (i + (k + ahead) // SLOTS + 1)

        block = ctx.enter_context(nc.Block())

        @block.sync
        def _(sp):
            sp.dma_start(key_i[:], src_cols).then_inc(S["keys_in"], 16)
            sp.dma_start(dst_i[:], dst_cols).then_inc(S["keys_in"], 16)
            for n, w in enumerate((w_in_s, w_in_v, w1_s[0:2 * C:2, :], w1_s[1:2 * C:2, :],
                                   w1_v[0:2 * C:2, :], w1_v[1:2 * C:2, :], w2_s, w2_v)):
                sp.dma_start(wraw[:, n, :], w).then_inc(S["weights_in"], 16)
            sp.dma_start(wf2_raw[:], wf2[:, 0:4 * C]).then_inc(S["weights_in"], 16)
            sp.dma_start(wf1_sb[:], wf1).then_inc(S["weights_in"], 16)
            sp.dma_start(bf1_sb[:], bf1.rearrange("(c a) -> c a", a=1)).then_inc(S["weights_in"], 16)
            for v in range(2):
                sp.dma_start(bf2_sb[:, 2 * v:2 * v + 2],
                             bf2[2 * C * v:2 * C * (v + 1)].rearrange("(c a) -> c a", a=2)).then_inc(S["weights_in"], 16)
            rows = src_rows.rearrange("(a n) -> a n", a=1)
            attr = attrs.rearrange("p (t w) -> p t w", w=ATTR)
            sp.wait_ge(S["consts"], 2)
            for h in range(2):
                sp.dma_start(keyrow[:, h, :], rows[:, h * (CHUNK * P):(h + 1) * (CHUNK * P)].to_broadcast([P, CHUNK * P])).then_inc(chunk_keys[h], 16)
                sp.dma_start(recs[:, h, :, 2:2 + ATTR], attr[:, h * CHUNK:(h + 1) * CHUNK, :]).then_inc(chunk_recs[h], 16)
            per = N_NODES // COPY_CHUNKS
            x5 = x.rearrange("(a b) c -> a (b c)", b=5)
            o5 = out.rearrange("(a b) c -> a (b c)", b=5)
            per = N_NODES // 5 // COPY_CHUNKS
            for c in range(COPY_CHUNKS - HALF + 1):
                sp.dma_start(o5[c * per:(c + 1) * per, :], x5[c * per:(c + 1) * per, :]).then_inc(S["copied"], 16)
            with sp.Fori(1, HALF) as i:
                for h in range(2):
                    c = 2 * i + h
                    sp.wait_ge(S["same_made"], (c - 1) * CHUNK + 2)
                    sp.dma_start(keyrow[:, h, :], rows[:, bass.ds(c * (CHUNK * P), CHUNK * P)].to_broadcast([P, CHUNK * P])).then_inc(chunk_keys[h], 16)
                    sp.wait_ge(chunk_out[h], i * (16 * CHUNK))
                    sp.dma_start(recs[:, h, :, 2:2 + ATTR], attr[:, bass.ds(c * CHUNK, CHUNK), :]).then_inc(chunk_recs[h], 16)
                n = i + (COPY_CHUNKS - HALF)
                sp.dma_start(o5[bass.ds(n * per, per), :], x5[bass.ds(n * per, per), :]).then_inc(S["copied"], 16)
            sp.wait_ge(S["pads_made"], 3)
            sp.dma_start(table[0:1, :], padrec[0:1, 0, :]).then_inc(S["pads_out"], 16)
            sp.dma_start(table[1 + SORTED:N_ROWS, :].rearrange("(p a) w -> p a w", a=PAD_ROWS), padrec[:]).then_inc(S["pads_out"], 16)
            sp.wait_ge(S["pads_out"], 32)
            for h in range(2):
                sp.wait_ge(chunk_out[h], 16 * CHUNK * HALF)

            def load_rec(g, slot):
                src = bass.AP(table.tensor, g * (GROUP * REAL * REC), [[REC, P], [REAL * REC, GROUP], [1, REC + 1]])
                sp.dma_start(rec[:, slot, :, :], src).then_inc(rec_in[slot], 16)

            for g in range(SLOTS):
                load_rec(g, g)
            with sp.Fori(0, N_LOOPS) as i:
                for k in range(SLOTS):
                    s = SLOTS * i + k
                    sp.wait_ge(S["sel_done"], s + 1)
                    sp.wait_ge(S["ft_ready"], s + 1)
                    sp.wait_ge(S["scale_made"], 2 * s + 2)
                    load_rec(s + SLOTS, k)
            for k in range(SLOTS):
                sp.wait_ge(rows_out[k], 16 * GROUP * len(range(k, N_GROUPS, SLOTS)))
            for k in range(2):
                sp.wait_ge(rec_in[(N_GROUPS + k) % SLOTS], 16 * (N_LOOPS + 1))

        @block.gpsimd
        def _(g):
            pool = nc.gpsimd
            pool.iota(iota_f[:], [[1, DIGIT]], base=0, channel_multiplier=0, allow_small_or_imprecise_dtypes=True).then_inc(S["iotas"], 1)
            pool.iota(iota_p[:], [[P, 2]], base=0, channel_multiplier=1, allow_small_or_imprecise_dtypes=True).then_inc(S["iotas"], 1)
            pool.memset(ones_m[:], 1.0).then_inc(S["consts"], 1)
            pool.memset(recs[:], 0.0).then_inc(S["consts"], 1)
            pool.memset(zeros_b[:], 0.0).then_inc(S["consts"], 1)
            g.wait_ge(S["consts"], 3)
            for m, sign, op in ((ident, 1, ALU.is_equal), (after, -1, ALU.is_gt), (before, 1, ALU.is_gt)):
                pool.affine_select(out=m[:], in_=ones_m[:], compare_op=op, fill=0.0, base=0,
                                   pattern=[[-sign, P]], channel_multiplier=sign).then_inc(S["consts"], 1)
            pool.memset(ones_f[:], 1.0).then_inc(S["consts"], 1)
            pool.memset(padrec[:], 1.0).then_inc(S["pads_made"], 1)
            g.wait_ge(S["pads_made"], 1)
            pool.memset(padrec[:, :, W_NODE], float(PAD_KEY)).then_inc(S["pads_made"], 1)
            pool.memset(padrec[:, :, W_SOURCE].bitcast(I32), 0).then_inc(S["pads_made"], 1)
            pool.memset(xs[:], 0.0).then_inc(S["zeroed"], 1)
            pool.memset(var[:], 1.0).then_inc(S["zeroed"], 1)
            last_row = g.to_reg(N_ROWS - 1)
            last_node = g.to_reg(N_NODES - 1)
            with g.Fori(0, HALF) as i:
                for h in range(2):
                    c = 2 * i + h
                    g.wait_ge(S["places_made"], c + 1)
                    g.sem_inc(S["pool_passed"], 1)
                    for j in range(CHUNK):
                        pool.indirect_dma_start(table, bass.IndirectOffsetOnAxis(ap=place_i[:, h, j:j + 1], axis=0),
                                                recs[:, h, j, :], None, bounds_check=last_row, oob_is_err=False).then_inc(chunk_out[h], 16)

            def step(s, i, k):
                q = (k + 3) % SLOTS
                n = s + 3
                if n < N_GROUPS + 1 if isinstance(n, int) else True:
                    g.wait_ge(rec_in[q], loads(i, k, 3, 1))
                    at_least(g, rows_out[q], loads(i, k, -1, GROUP))
                    node, following = rec[:, q, :, W_NODE], rec[:, q, :, REC]
                    pool.tensor_tensor(idx_f[:, 0, :], following, node, ALU.subtract).then_inc(S["idx_made"], 1)
                    wait_apart(g, S["idx_made"], 5 * n + 1, S["pool_passed"])
                    pool.tensor_scalar(idx_f[:, 1, :], idx_f[:, 0, :], 1.0, -SKIP, ALU.min, ALU.mult).then_inc(S["idx_made"], 1)
                    g.wait_ge(S["idx_made"], 5 * n + 2)
                    pool.tensor_tensor(idx_f[:, 2, :], idx_f[:, 1, :], node, ALU.add).then_inc(S["idx_made"], 1)
                    wait_apart(g, S["idx_made"], 5 * n + 3, S["pool_passed"])
                    pool.tensor_scalar(scat_i[:, q, :], idx_f[:, 2, :], SKIP, None, ALU.add).then_inc(S["idx_made"], 1)
                    wait_apart(g, S["idx_made"], 5 * n + 4, S["pool_passed"])
                    pool.memset(scat_i[0:1, q, :], int(SKIP)).then_inc(S["idx_made"], 1)
                    at_least(g, S["t_ready"], 5 * s)
                    g.sem_inc(S["pool_passed"], 1)
                    for j in range(GROUP):
                        pool.indirect_dma_start(xg[:, q, j, :], None, x,
                                                bass.IndirectOffsetOnAxis(ap=rec[:, q, j, W_SOURCE:W_SOURCE + 1].bitcast(I32), axis=0),
                                                bounds_check=last_node, oob_is_err=False).then_inc(xg_in[q], 16)
                    vec = rec[:, q, :, W_VEC:W_VEC + 3]
                    at_least(g, S["rsq_made"], 2 * n)
                    pool.tensor_tensor(sq[:], vec, vec, ALU.mult).then_inc(S["squares"], 1)
                    g.wait_ge(S["squares"], 3 * n + 1)
                    pool.tensor_tensor(sq_sum[:], sq[:, :, 0], sq[:, :, 1], ALU.add).then_inc(S["squares"], 1)
                    g.wait_ge(S["squares"], 3 * n + 2)
                    at_least(g, S["newton"], 4 * n)
                    pool.tensor_tensor(var[:, 4:8], sq_sum[:], sq[:, :, 2], ALU.add).then_inc(S["squares"], 1)
                p = s + 2
                if not isinstance(p, int) or 0 <= p < N_GROUPS:
                    z = (k + 2) % SLOTS
                    at_least(g, rows_out[z], loads(i, k, -2, GROUP))
                    at_least(g, S["idx_made"], 5 * p + 5)
                    g.sem_inc(S["pool_passed"], 1)
                    for j in range(GROUP):
                        pool.indirect_dma_start(xs[:, z, j, :], None, x,
                                                bass.IndirectOffsetOnAxis(ap=scat_i[:, z, j:j + 1], axis=0),
                                                bounds_check=last_node, oob_is_err=False).then_inc(xs_in[z], 16)
                if not isinstance(p, int) or p < N_GROUPS:
                    g.wait_ge(S["rsq_made"], 2 * n + 2)
                    pool.tensor_tensor(newt[:, 0, :], rsq[:, 1, :], rsq[:, 1, :], ALU.mult).then_inc(S["newton"], 1)
                    g.wait_ge(S["newton"], 4 * n + 1)
                    pool.tensor_tensor(newt[:, 1, :], newt[:, 0, :], var[:], ALU.mult).then_inc(S["newton"], 1)
                    wait_apart(g, S["newton"], 4 * n + 2, S["pool_passed"])
                    pool.tensor_scalar(newt[:, 2, :], newt[:, 1, :], -0.5, 1.5, ALU.mult, ALU.add).then_inc(S["newton"], 1)
                    g.wait_ge(S["newton"], 4 * n + 3)
                    at_least(g, S["unit_made"], n)
                    pool.tensor_tensor(newt[:, 3, :], newt[:, 2, :], rsq[:, 1, :], ALU.mult).then_inc(S["newton"], 1)
                    g.wait_ge(S["newton"], 4 * n + 4)
                    at_least(g, S["y_made"], 4 * s)
                    pool.tensor_tensor(unit[:, q, :, :], rec[:, q, :, W_VEC:W_VEC + 3],
                                       newt[:, 3, 4:8].rearrange("p (g a) -> p g a", a=1).to_broadcast([P, GROUP, 3]),
                                       ALU.mult).then_inc(S["unit_made"], 1)
                    if not isinstance(p, int) or p >= 0:
                        z = (k + 2) % SLOTS
                        at_least(g, S["sel_done"], s + 1)
                        pool.tensor_tensor(scale[:, k % 2, :], newt[:, 3, 0:4], rec[:, z, :, W_WEIGHT], ALU.mult).then_inc(S["scale_made"], 1)
                        wait_apart(g, S["scale_made"], 2 * p + 1, S["pool_passed"])
                        pool.memset(scale[0:1, k % 2, :], 1.0).then_inc(S["scale_made"], 1)
                if not isinstance(s, int) or s >= 0:
                    g.wait_ge(S["s_added"], s + 1)
                    g.wait_ge(S["copied"], 16 * COPY_CHUNKS)
                    g.sem_inc(S["pool_passed"], 1)
                    for j in range(GROUP):
                        pool.indirect_dma_start(out, bass.IndirectOffsetOnAxis(ap=scat_i[:, k, j:j + 1], axis=0),
                                                xs[:, k, j, :], None, bounds_check=last_node, oob_is_err=False).then_inc(rows_out[k], 16)

            g.wait_ge(S["zeroed"], 2)
            steps(g, step, -3)
            g.wait_ge(xg_in[N_GROUPS % SLOTS], 16 * GROUP * (N_LOOPS + 1))

        @block.scalar
        def _(a):
            act = nc.scalar.activation
            root = 1.0 / math.sqrt(C)
            mix = 1.0 / math.sqrt(2 * C)
            a.wait_ge(S["weights_in"], 16 * 13)
            for n, (dst, src, factor) in enumerate((
                    (w_a, wraw[:, 0, :], root), (w_b, wraw[:, 1, :], root),
                    (m_a, wraw[:, 2, :], mix * Y0), (m_b, wraw[:, 3, :], mix * Y1_SCALE / math.sqrt(3.0)),
                    (w2_sb, wraw[:, 6, :], root))):
                act(dst[:], src, ACT.Copy, scale=factor).then_inc(S["weights_made"], 1)
            for v in range(2):
                for b in range(2):
                    cols = wf2_raw[:, 2 * C * v:2 * C * (v + 1)].rearrange("p (c a) -> p a c", a=2)[:, b, :]
                    act(wf2_sb[:, 2 * v + b, :], cols, ACT.Copy).then_inc(S["weights_made"], 1)
            a.wait_ge(S["weights_t"], 1)
            act(w_t[:], b_sq[:, 0:2 * C].rearrange("p (a c) -> p a c", a=2), ACT.Copy).then_inc(S["weights_tc"], 1)
            a.wait_ge(S["weights_u"], 1)
            act(u_c[:], b_z[:, 0:C], ACT.Copy, scale=mix * root * Y1_SCALE).then_inc(S["weights_made"], 1)
            act(u_d[:], b_z[:, C:2 * C], ACT.Copy, scale=mix * root * Y0).then_inc(S["weights_made"], 1)

            with a.Fori(0, HALF) as i:
                for k in range(2 * CHUNK):
                    t = i * (2 * CHUNK) + k
                    a.wait_ge(S["counts_moved"], t + 1)
                    a.wait_ge(S["looked_up"], t + 1)
                    act(counts_sb[:, k % 2, :, :], counts_ps[:].rearrange("p (a b) -> p a b", a=2), ACT.Copy).then_inc(S["counts_read"], 1)

            def t_copy(f, i):
                a.wait_ge(S["t_ready"], 5 * f + i + 1)
                at_least(a, S["j_ready"], 5 * f)
                act(h_t[:, i, :], FB[(3 + i) % 4][:], ACT.Copy).then_inc(S["t_copied"], 1)

            def w_copy(f, i):
                bank, bias = ((0, 0), (1, 2), (3, 1), (1, 3))[i]
                a.wait_ge(S["w_ready"], 4 * f + i + 1)
                at_least(a, S["prod_done"], 6 * f)
                act(w_sb[:, i, :], FB[bank][:], ACT.Identity, bias=bf2_sb[:, bias:bias + 1]).then_inc(S["w_copied"], 1)

            def sq_copy(b, k, j):
                a.wait_ge(S["sq_ready"], 4 * b + j + 1)
                act(y[:, k % 2, j, 0:C], b_sq[:, 0:C], ACT.Copy).then_inc(S["ys_made"], 1)
                act(zq[:, j % 2, :], b_sq[:, C:2 * C], ACT.Copy).then_inc(S["sq_copied"], 1)

            def s_copy(b, j):
                a.wait_ge(S["seg_ready"], 4 * b + j + 1)
                at_least(a, S["st_ready"], b)
                act(s_sb[:, j, :], b_seg[:, 0:C], ACT.Copy).then_inc(S["s_copied"], 1)

            def carry(t, par, j):
                a.wait_ge(S["v_added"], t + 1)
                a.wait_ge(S["y_made"], t + 2)
                a.wait_ge(S["ys_made"], t + 2)
                act(y[0:1, par, j, :], b_seg[0:1, :], ACT.Copy).then_inc(S["carried"], 1)

            def step(s, i, k):
                b, f, n = s, s + 1, s + 3
                known = isinstance(s, int)
                back, front, pre = (not known or s >= 0), (not known or 0 <= s + 1 < N_GROUPS), (not known or s + 2 < N_GROUPS)
                if front:
                    a.wait_ge(S["ft_ready"], f + 1)
                    at_least(a, S["h1_ready"], f)
                    act(ft_sb[:], FB[1][0:N_RBF, :], ACT.Copy).then_inc(S["ft_copied"], 1)
                if back:
                    sq_copy(b, k, 0)
                    carry(4 * b - 1, k % 2, 0)
                if front:
                    a.wait_ge(S["h1_ready"], f + 1)
                    at_least(a, S["f_exp"], f)
                    act(fa[:, 0, :], FB[2][:], ACT.Abs, bias=bf1_sb[:]).then_inc(S["f_abs"], 1)
                    at_least(a, S["sp_done"], f)
                    act(fr[:], FB[2][:], ACT.Relu, bias=bf1_sb[:]).then_inc(S["h1_read"], 1)
                    a.wait_ge(S["f_abs"], f + 1)
                    at_least(a, S["f_ln"], f)
                    act(fa[:, 1, :], fa[:, 0, :], ACT.Exp, scale=-1.0).then_inc(S["f_exp"], 1)
                    t_copy(f, 0)
                    a.wait_ge(S["f_exp"], f + 1)
                    act(fa[:, 2, :], fa[:, 1, :], ACT.Ln, bias=1.0).then_inc(S["f_ln"], 1)
                if back:
                    sq_copy(b, k, 1)
                    s_copy(b, 0)
                    carry(4 * b, k % 2, 1)
                if front:
                    t_copy(f, 1)
                    t_copy(f, 2)
                if back:
                    sq_copy(b, k, 2)
                    s_copy(b, 1)
                    carry(4 * b + 1, k % 2, 2)
                if pre:
                    at_least(a, S["var_made"], s + 3)
                    a.wait_ge(S["squares"], 3 * n + 3)
                    at_least(a, S["rsq_made"], 2 * n)
                    act(rsq[:, 0, :], var[:], ACT.Ln).then_inc(S["rsq_made"], 1)
                    a.wait_ge(S["rsq_made"], 2 * n + 1)
                    at_least(a, S["newton"], 4 * n)
                    act(rsq[:, 1, :], rsq[:, 0, :], ACT.Exp, scale=-0.5).then_inc(S["rsq_made"], 1)
                if front:
                    t_copy(f, 3)
                    t_copy(f, 4)
                if back:
                    sq_copy(b, k, 3)
                    s_copy(b, 2)
                    carry(4 * b + 2, k % 2, 3)
                if front:
                    w_copy(f, 0)
                    w_copy(f, 1)
                if back:
                    s_copy(b, 3)
                    a.wait_ge(S["st_ready"], b + 1)
                    at_least(a, S["b_exp"], b)
                    act(ba[:, 0, :], b_s[:], ACT.Abs).then_inc(S["b_abs"], 1)
                    at_least(a, S["ssp_done"], b)
                    act(br[:], b_s[:], ACT.Relu).then_inc(S["st_read"], 1)
                    a.wait_ge(S["b_abs"], b + 1)
                    at_least(a, S["b_ln"], b)
                    act(ba[:, 1, :], ba[:, 0, :], ACT.Exp, scale=-1.0).then_inc(S["b_exp"], 1)
                if front:
                    w_copy(f, 2)
                if back:
                    a.wait_ge(S["b_exp"], b + 1)
                    act(ba[:, 2, :], ba[:, 1, :], ACT.Ln, bias=1.0).then_inc(S["b_ln"], 1)
                if front:
                    w_copy(f, 3)

            a.wait_ge(S["zeroed"], 2)
            a.wait_ge(S["carry_start"], 1)
            steps(a, step, -3)

        @block.tensor
        def _(pe):
            mm, tr = nc.tensor.matmul, nc.tensor.transpose
            pe.wait_ge(S["consts"], 7)
            pe.wait_ge(S["weights_in"], 16 * 13)
            tr(b_sq[:, 0:C], wraw[:, 4, :], ident[:])
            tr(b_sq[:, C:2 * C], wraw[:, 5, :], ident[:]).then_inc(S["weights_t"], 1)
            pe.wait_ge(S["weights_tc"], 1)
            mm(b_z[:, 0:C], w_t[:, 0, :], wraw[:, 7, :], start=True, stop=True)
            mm(b_z[:, C:2 * C], w_t[:, 1, :], wraw[:, 7, :], start=True, stop=True).then_inc(S["weights_u"], 1)

            def add_counts(slot):
                for c in range(2):
                    m = mm(counts_ps[:, DIGIT * c:DIGIT * (c + 1)], onehot[:, slot, 0, P * c:P * (c + 1)], onehot[:, slot, 1, :],
                           start=False, stop=False, skip_group_check=True)
                return m

            pe.sem_inc(S["onehots_free"], BF_SLOTS)
            pe.sem_inc(S["looked_up"], 2)
            mm(counts_ps[:, 0:DIGIT], zeros_b[:, 0:P], zeros_b[:], start=True, stop=False, skip_group_check=True)
            mm(counts_ps[:, DIGIT:2 * DIGIT], zeros_b[:, 0:P], zeros_b[:], start=False, stop=False, skip_group_check=True)
            with pe.Fori(0, RANK_TILES // BF_SLOTS) as i:
                for k in range(BF_SLOTS):
                    pe.wait_ge(S["onehots_made"], i * BF_SLOTS + k + 1)
                    add_counts(k).then_inc(S["onehots_free"], 1)
            pe.wait_ge(S["totals_made"], 1)
            mm(off_ps[:, 0:1], after[:], row_total[:, 0:1], start=True, stop=True)
            mm(off_ps[:, 1:2], after[:], row_total[:, 1:2], start=True, stop=False)
            mm(off_ps[:, 1:2], ones_m[:], row_total[:, 0:1], start=False, stop=True).then_inc(S["offsets_made"], 1)
            pe.wait_ge(S["base_made"], 1)
            mm(counts_ps[:], ident[:], base.rearrange("p a b -> p (a b)"), start=True, stop=False, skip_group_check=True).then_inc(S["counts_moved"], 1)
            with pe.Fori(0, N_CHUNKS // UNROLL) as i:
                for k in range(UNROLL * CHUNK):
                    t = i * (UNROLL * CHUNK) + k
                    pe.wait_ge(S["counts_read"], t + 1)
                    pe.wait_ge(S["onehots_made"], RANK_TILES + t + 1)
                    add_counts(k % BF_SLOTS).then_inc(S["counts_moved"], 1)
                    if k % CHUNK == 0:
                        pe.wait_ge(S["onehot_t_made"], UNROLL * i + k // CHUNK + 1)
                    pe.wait_ge(S["look_free"], t + 1)
                    h, j = (k // CHUNK) % 2, k % CHUNK
                    for c in range(2):
                        m = mm(look_ps[k % 2][:, 0:DIGIT], onehot_t[:, h, c, j * P:(j + 1) * P], counts_sb[:, k % 2, c, :],
                               start=(c == 0), stop=(c == 1))
                    m.then_inc(S["looked_up"], 1)

            def step(s, i, k):
                b, f = s, s + 1
                known = isinstance(s, int)
                back, front = (not known or s >= 0), (not known or 0 <= s + 1 < N_GROUPS)
                q = (k + 1) % SLOTS
                fp, bp = (k + 1) % 2, k % 2
                tile = [slice(j * P, (j + 1) * P) for j in range(GROUP)]

                def t_item(n):
                    bank = FB[(3 + n) % 4]
                    for j in range(GROUP):
                        if n == 4:
                            src = gsum[:, fp, 2, j, :]
                        elif n == 0:
                            src = xg[:, q, j, 0:C]
                        else:
                            src = xg[:, q, j, C:D].rearrange("p (c i) -> p i c", i=3)[:, n - 1, :]
                        m = tr(bank[:, tile[j]], src, ident[:])
                    m.then_inc(S["t_ready"], 1)

                def w_item(n):
                    bank, col = ((0, 0), (1, 2), (3, 1), (1, 3))[n]
                    mm(FB[bank][:], wf2_sb[:, col, :], sp_t[:], start=True, stop=True).then_inc(S["w_ready"], 1)

                def j_item(bank, w, n):
                    mm(FB[bank][:], w[:], h_t[:, n, :], start=True, stop=True).then_inc(S["j_ready"], 1)

                def messages(j):
                    at_least(pe, S["sq_copied"], 4 * b + j)
                    mm(b_sq[:, 0:C], prod[:, bp, 0, tile[j]], m_a[:], start=True, stop=False)
                    mm(b_sq[:, 0:C], prod[:, bp, 2, tile[j]], m_b[:], start=False, stop=True)
                    mm(b_sq[:, C:2 * C], prod[:, bp, 1, tile[j]], u_c[:], start=True, stop=True).then_inc(S["sq_ready"], 1)
                    at_least(pe, S["y_made"], 4 * b + j)
                    for c in range(3):
                        m = mm(b_z[:, c * C:(c + 1) * C], prod[:, bp, 3 + c, tile[j]], u_d[:], start=True, stop=True)
                    m.then_inc(S["z_ready"], 1)

                def segment(j):
                    pe.wait_ge(S["y_made"], 4 * b + j + 1)
                    pe.wait_ge(S["carried"], 4 * b + j + 1)
                    mm(b_seg[:], sel[:, bp, j, :], y[:, bp, j, :], start=True, stop=True).then_inc(S["seg_ready"], 1)

                if front:
                    pe.wait_ge(rec_in[q], loads(i, k, 1, 1))
                    at_least(pe, S["prod_done"], 6 * f)
                    for j in range(GROUP):
                        m = tr(FB[0][:, tile[j]], rec[:, q, j, W_NODE:W_NODE + 1].to_broadcast([P, P]), ident[:])
                    m.then_inc(S["keyb_ready"], 1)
                    at_least(pe, S["w_copied"], 4 * f)
                    for j in range(GROUP):
                        m = tr(FB[1][0:N_RBF, tile[j]], rec[:, q, j, W_RBF:W_RBF + N_RBF], ident[:])
                    m.then_inc(S["ft_ready"], 1)
                if back:
                    pe.wait_ge(S["prod_done"], 6 * b + 6)
                    messages(0)
                if front:
                    pe.wait_ge(S["ft_copied"], f + 1)
                    mm(FB[2][:], wf1_sb[:], ft_sb[:], start=True, stop=True).then_inc(S["h1_ready"], 1)
                    pe.wait_ge(S["pre_made"], 4 * f + 4)
                    t_item(0)
                if back:
                    messages(1)
                    pe.wait_ge(S["sel_done"], b + 1)
                    segment(0)
                if front:
                    pe.wait_ge(S["sel_made"], 4 * f + 4)
                    t_item(1)
                    pe.wait_ge(S["ft_copied"], f + 1)
                    t_item(2)
                if back:
                    messages(2)
                    segment(1)
                if front:
                    pe.wait_ge(S["h1_read"], f + 1)
                    t_item(3)
                    pe.wait_ge(S["t_copied"], 5 * f + 1)
                    t_item(4)
                if back:
                    messages(3)
                    segment(2)
                if front:
                    pe.wait_ge(S["sp_done"], f + 1)
                    pe.wait_ge(S["t_copied"], 5 * f + 2)
                    w_item(0)
                    pe.wait_ge(S["t_copied"], 5 * f + 3)
                    w_item(1)
                if back:
                    segment(3)
                if front:
                    pe.wait_ge(S["t_copied"], 5 * f + 4)
                    j_item(2, w_a, 0)
                if back:
                    pe.wait_ge(S["s_copied"], 4 * b + 4)
                    at_least(pe, S["s_added"], b)
                    for j in range(GROUP):
                        m = tr(b_s[:, tile[j]], s_sb[:, j, :], ident[:])
                    m.then_inc(S["st_ready"], 1)
                if front:
                    pe.wait_ge(S["t_copied"], 5 * f + 5)
                    w_item(2)
                    pe.wait_ge(S["w_copied"], 4 * f + 1)
                    j_item(0, w_b, 4)
                    pe.wait_ge(S["w_copied"], 4 * f + 2)
                    w_item(3)
                    pe.wait_ge(S["prod_done"], 6 * f + 2)
                    j_item(2, w_b, 1)
                    pe.wait_ge(S["w_copied"], 4 * f + 3)
                    j_item(3, w_b, 2)
                    pe.wait_ge(S["prod_done"], 6 * f + 3)
                    j_item(0, w_b, 3)
                if back:
                    pe.wait_ge(S["ssp_done"], b + 1)
                    pe.wait_ge(S["st_read"], b + 1)
                    for j in range(GROUP):
                        m = mm(b_s[:, tile[j]], ssp_t[:, tile[j]], w2_sb[:], start=True, stop=True)
                    m.then_inc(S["s2_ready"], 1)

            pe.wait_ge(S["weights_made"], 11)
            mm(b_seg[:, 0:DIGIT], zeros_b[:, 0:P], zeros_b[:], start=True, stop=True)
            mm(b_seg[:, DIGIT:2 * DIGIT], zeros_b[:, 0:P], zeros_b[:], start=True, stop=True).then_inc(S["carry_start"], 1)
            steps(pe, step, -1)

        @block.vector
        def _(d):
            v = nc.vector
            d.sem_inc(S["look_free"], 2)
            d.sem_inc(S["same_made"], 2)
            d.wait_ge(S["keys_in"], 32)
            v.tensor_single_scalar(digit_i[:, 0, :], key_i[:], 8, ALU.arith_shift_right).then_inc(S["digits_made"], 1)
            v.tensor_single_scalar(digit_i[:, 1, :], key_i[:], DIGIT - 1, ALU.bitwise_and).then_inc(S["digits_made"], 1)
            d.wait_ge(S["iotas"], 2)
            v.tensor_copy(iota_b[:], iota_f[:]).then_inc(S["digits_made"], 1)
            v.tensor_copy(digits[:, 2, :], key_i[:]).then_inc(S["digits_made"], 1)
            d.wait_ge(S["digits_made"], 4)
            v.tensor_copy(digits[:, 0:2, :], digit_i[:]).then_inc(S["digits_made"], 1)
            d.wait_ge(S["digits_made"], 5)

            def onehots(slot, h, j):
                for c in range(2):
                    m = v.tensor_scalar(onehot[:, slot, c, :], iota_b[:], dig[:, h, c, j:j + 1], None, ALU.is_equal)
                m.then_inc(S["onehots_made"], 1)

            with d.Fori(0, N_CHUNKS // UNROLL) as i:
                for hh in range(UNROLL):
                    c = UNROLL * i + hh
                    h = hh % 2
                    v.tensor_copy(dig[:, h, :, :], digits[:, :, bass.ds(c * CHUNK, CHUNK)]).then_inc(S["dig_made"], 1)
                    d.wait_ge(S["dig_made"], c + 1)
                    for j in range(CHUNK):
                        d.wait_ge(S["onehots_free"], c * CHUNK + j + 1)
                        onehots((hh * CHUNK + j) % BF_SLOTS, h, j)
            d.wait_ge(S["onehots_free"], RANK_TILES + BF_SLOTS)
            v.tensor_copy(count.rearrange("p a b -> p (a b)"), counts_ps[:]).then_inc(S["hist_step"], 1)
            d.wait_ge(S["hist_step"], 1)
            d.wait_ge(S["consts"], 7)
            for c in range(2):
                v.tensor_tensor_scan(upto[:, c, :], ones_f[:], count[:, c, :], 0.0, ALU.mult, ALU.add).then_inc(S["hist_step"], 1)
            d.wait_ge(S["hist_step"], 3)
            v.tensor_copy(row_total[:], upto[:, :, DIGIT - 1]).then_inc(S["totals_made"], 1)
            d.wait_ge(S["totals_made"], 1)
            v.tensor_tensor(upto, upto, count, ALU.subtract).then_inc(S["hist_step"], 1)
            d.wait_ge(S["offsets_made"], 1)
            v.tensor_scalar(row_base[:], off_ps[:, 0:2], 1.0, None, ALU.add).then_inc(S["hist_step"], 1)
            d.wait_ge(S["hist_step"], 5)
            for c in range(2):
                m = v.tensor_scalar(base[:, c, :], upto[:, c, :], row_base[:, c:c + 1], None, ALU.add)
            m.then_inc(S["base_made"], 1)

            def look(slot, h, j, t):
                d.wait_ge(S["looked_up"], t + 3)
                d.wait_ge(S["look_free"], t + 1)
                v.scalar_tensor_tensor(out=junk_look[:, slot, :], in0=iota_f[:], scalar=dig[:, h, 1, j:j + 1],
                                       in1=look_ps[slot][:, 0:DIGIT], op0=ALU.is_equal, op1=ALU.mult,
                                       accum_out=looked[:, h, j:j + 1]).then_inc(S["look_free"], 1)

            def places(c, h):
                d.wait_ge(S["look_free"], (c + 1) * CHUNK + 2)
                v.tensor_tensor(place[:], looked[:, h, :], same[:, h, :], ALU.add).then_inc(S["place_summed"], 1)
                d.wait_ge(S["place_summed"], c + 1)
                v.tensor_copy(place_i[:, h, :], place[:]).then_inc(S["places_made"], 1)

            def chunks(i, first=False):
                for hh in range(UNROLL):
                    c = UNROLL * i + hh
                    h = hh % 2
                    v.tensor_copy(dig[:, h, :, :], digits[:, :, bass.ds(c * CHUNK, CHUNK)]).then_inc(S["dig_made"], 1)
                    d.wait_ge(chunk_keys[h], 16 * (2 * i + hh // 2 + 1))
                    v.tensor_single_scalar(hirow, keyrow[:, h, :], 8, ALU.arith_shift_right).then_inc(S["hirow_made"], 1)
                    d.wait_ge(chunk_recs[h], 16 * (2 * i + hh // 2 + 1))
                    v.tensor_copy(recs[:, h, :, W_NODE], digits[:, 2, bass.ds(c * CHUNK, CHUNK)])
                    v.tensor_copy(recs[:, h, :, W_SOURCE].bitcast(I32), dst_i[:, bass.ds(c * CHUNK, CHUNK)])
                    d.wait_ge(S["hirow_made"], c + 1)
                    d.wait_ge(S["dig_made"], N_CHUNKS + c + 1)
                    for q in range(2):
                        m = v.tensor_scalar(onehot_t[:, h, q, :], hirow, iota_p[:, q:q + 1], None, ALU.is_equal)
                    m.then_inc(S["onehot_t_made"], 1)
                    for j in range(CHUNK):
                        k = hh * CHUNK + j
                        t = c * CHUNK + j
                        if not (first and k < BF_SLOTS - 1):
                            d.wait_ge(S["counts_moved"], t - 2)
                        onehots(k % BF_SLOTS, h, j)
                        d.wait_ge(S["same_made"], t + 1)
                        v.scalar_tensor_tensor(out=junk_same[:, k % 2, :], in0=keyrow[:, h, j * P:(j + 1) * P], scalar=dig[:, h, 2, j:j + 1],
                                               in1=before[:], op0=ALU.is_equal, op1=ALU.mult, accum_out=same[:, h, j:j + 1]).then_inc(S["same_made"], 1)
                        if not (first and k < LAG):
                            kk = (k - LAG) % (UNROLL * CHUNK)
                            look(kk % 2, (kk // CHUNK) % 2, kk % CHUNK, t - LAG)
                        if j == LAG - 1 and not (first and hh == 0):
                            places(c - 1, 1 - h)

            chunks(0, first=True)
            with d.Fori(1, N_CHUNKS // UNROLL) as i:
                chunks(i)
            for k in range(UNROLL * CHUNK - LAG, UNROLL * CHUNK):
                look(k % 2, (k // CHUNK) % 2, k % CHUNK, RANK_TILES - UNROLL * CHUNK + k)
            places(N_CHUNKS - 1, 1)

            def step(s, i, k):
                b, f, p = s, s + 1, s + 2
                known = isinstance(s, int)
                back, front, pre = (not known or s >= 0), (not known or 0 <= s + 1 < N_GROUPS), (not known or s + 2 < N_GROUPS)
                fp, bp = (k + 1) % 2, k % 2
                q, z = (k + 1) % SLOTS, (k + 2) % SLOTS
                hv = [xg[:, z, j, C:D].rearrange("p (c i) -> p i c", i=3) for j in range(GROUP)]

                def combine(j):
                    d.wait_ge(S["z_ready"], 4 * b + j + 1)
                    d.wait_ge(S["sq_copied"], 4 * b + j + 1)
                    for c in range(3):
                        m = v.scalar_tensor_tensor(out=y[:, bp, j, (c + 1) * C:(c + 2) * C], in0=zq[:, j % 2, :], scalar=unit[:, k, j, c:c + 1],
                                                   in1=b_z[:, c * C:(c + 1) * C], op0=ALU.mult, op1=ALU.add)
                    m.then_inc(S["y_made"], 1)

                def add_vectors(j):
                    if j == 0:
                        d.wait_ge(xs_in[k], loads(i, k, 0, GROUP))
                    d.wait_ge(S["s_copied"], 4 * b + j + 1)
                    xv = xs[:, k, j, C:D].rearrange("p (c i) -> p i c", i=3)
                    v.tensor_tensor(xv, b_seg[:, C:D].rearrange("p (i c) -> p i c", i=3), xv, ALU.add).then_inc(S["v_added"], 1)

                def product(n, bank, w):
                    v.tensor_tensor(prod[:, fp, n, :], FB[bank][:], w_sb[:, w, :], ALU.mult).then_inc(S["prod_done"], 1)

                def projected(c):
                    for j in range(GROUP):
                        if c == 0:
                            d.wait_ge(S["h_made"], 4 * p + j + 1)
                            v.tensor_scalar(gsum[:, bp, 0, j, :], hv[j][:, 0, :], unit[:, z, j, 0:1], None, ALU.mult).then_inc(S["g_part"], 1)
                        else:
                            d.wait_ge(S["g_part"], 8 * p + 4 * (c - 1) + j + 1)
                            m = v.scalar_tensor_tensor(out=gsum[:, bp, c, j, :], in0=hv[j][:, c, :], scalar=unit[:, z, j, c:c + 1],
                                                       in1=gsum[:, bp, c - 1, j, :], op0=ALU.mult, op1=ALU.add)
                            m.then_inc(S["pre_made"] if c == 2 else S["g_part"], 1)

                if pre:
                    d.wait_ge(xg_in[z], loads(i, k, 2, GROUP))
                    at_least(d, S["mv_made"], 4 * p)
                    for j in range(GROUP):
                        v.bn_stats(stats[:, j, :], xg[:, z, j, :]).then_inc(S["stats_made"], 1)
                    at_least(d, S["h_made"], 4 * p)
                    at_least(d, S["var_made"], p)
                    wait_apart(d, S["stats_made"], 4 * p + 4, S["dve_passed"])
                    for j in range(GROUP):
                        v.bn_aggr(mv[:, j, :], stats[:, j, :]).then_inc(S["mv_made"], 1)
                if front:
                    d.wait_ge(S["keyb_ready"], f + 1)
                    d.wait_ge(S["scale_made"], 2 * f + 2)
                    at_least(d, S["seg_ready"], 4 * (f - 1))
                    for j in range(GROUP):
                        v.tensor_scalar(sel[:, fp, j, :], FB[0][:, j * P:(j + 1) * P], rec[:, q, j, W_NODE:W_NODE + 1],
                                        scale[:, fp, j:j + 1], ALU.is_equal, ALU.mult).then_inc(S["sel_made"], 1)
                if pre:
                    d.wait_ge(S["mv_made"], 4 * p + 4)
                    d.wait_ge(S["newton"], 4 * (s + 3))
                    v.tensor_scalar(var[:, 0:4], mv[:, :, 1], EPS, None, ALU.add).then_inc(S["var_made"], 1)
                if front:
                    d.wait_ge(S["sel_made"], 4 * f + 4)
                    v.tensor_copy(sel[:, fp, :, 0:1], sel[:, fp, :, P - 1:P]).then_inc(S["sel_done"], 1)
                if back:
                    combine(0)
                if pre:
                    d.wait_ge(S["mv_made"], 4 * p + 4)
                    for j in range(GROUP):
                        v.tensor_scalar(xg[:, z, j, :], xg[:, z, j, :], mv[:, j, 0:1], 0.0, ALU.subtract, ALU.max).then_inc(S["h_made"], 1)
                if front:
                    d.wait_ge(S["f_ln"], f + 1)
                    at_least(d, S["w_ready"], 4 * f)
                    v.scalar_tensor_tensor(out=sp_t[:], in0=fr[:], scalar=-LOG2, in1=fa[:, 2, :], op0=ALU.add, op1=ALU.add).then_inc(S["sp_done"], 1)
                if back:
                    combine(1)
                    add_vectors(0)
                if pre:
                    d.wait_ge(S["unit_made"], p + 1)
                    at_least(d, S["t_ready"], 5 * (p - 1))
                    projected(0)
                if back:
                    combine(2)
                    add_vectors(1)
                if pre:
                    projected(1)
                if back:
                    combine(3)
                    add_vectors(2)
                if front:
                    d.wait_ge(S["j_ready"], 5 * f + 1)
                    at_least(d, S["z_ready"], 4 * (f - 1))
                    d.wait_ge(S["w_copied"], 4 * f + 1)
                    product(0, 2, 0)
                    d.wait_ge(S["w_copied"], 4 * f + 2)
                    product(1, 2, 1)
                if back:
                    add_vectors(3)
                if pre:
                    projected(2)
                if front:
                    d.wait_ge(S["j_ready"], 5 * f + 2)
                    d.wait_ge(S["w_copied"], 4 * f + 3)
                    product(2, 0, 2)
                if back:
                    d.wait_ge(S["b_ln"], b + 1)
                    at_least(d, S["s2_ready"], b)
                    v.scalar_tensor_tensor(out=ssp_t[:], in0=br[:], scalar=-LOG2, in1=ba[:, 2, :], op0=ALU.add, op1=ALU.add).then_inc(S["ssp_done"], 1)
                if front:
                    d.wait_ge(S["w_copied"], 4 * f + 4)
                    for n, bank in ((0, 2), (1, 3), (2, 0)):
                        d.wait_ge(S["j_ready"], 5 * f + 3 + n)
                        product(3 + n, bank, 3)
                if back:
                    d.wait_ge(S["s2_ready"], b + 1)
                    v.tensor_tensor(xs[:, k, :, 0:C], b_s[:].rearrange("p (g c) -> p g c", g=GROUP), xs[:, k, :, 0:C], ALU.add).then_inc(S["s_added"], 1)

            steps(d, step, -2)


_OUTS = [((N_NODES, D), "float32")]


def kernel(**inputs):
    import numpy as _np
    import concourse.bacc as _bacc
    from concourse import mybir as _mybir
    from concourse.bass_utils import run_bass_kernel_spmd as _run

    a = {k: _np.asarray(v) for k, v in inputs.items()}
    pad = RANK_TILES * P - N_EDGES
    src = _np.concatenate([a["src"].astype(_np.int32), _np.full(pad, PAD_KEY, _np.int32)]).reshape(P, RANK_TILES)
    dst = _np.concatenate([a["dst"].astype(_np.int32), _np.zeros(pad, _np.int32)]).reshape(P, RANK_TILES)
    attrs = _np.concatenate([a["edge_weight"][:, None], a["edge_attr_3"], a["edge_attr_20"]], axis=1)
    attrs = _np.concatenate([attrs, _np.ones((pad, ATTR), _np.float32)]).reshape(P, RANK_TILES * ATTR)
    given = {
        "x": a["x"], "src_cols": src, "src_rows": src.T.reshape(-1), "dst_cols": dst, "attrs": attrs,
        **{n: a["L0_gnn_" + n] for n in ("W_in2f_s", "W_in2f_v", "Wf1", "bf1", "Wf2", "bf2", "W1_s", "W1_v", "W2_s", "W2_v")},
    }
    nc = _bacc.Bacc("TRN2", target_bir_lowering=False, num_devices=1)
    arrays, args = {}, []
    for name, value in given.items():
        value = _np.ascontiguousarray(value)
        arrays[f"in_{name}_dram"] = value
        args.append(nc.dram_tensor(f"in_{name}_dram", value.shape, _mybir.dt.from_np(value.dtype), kind="ExternalInput").ap())
    for i, (shape, dtype) in enumerate(_OUTS):
        dt = _mybir.dt.from_np(_np.dtype(dtype))
        args.append(nc.dram_tensor(f"out_{i}_dram", shape, dt, kind="ExternalOutput").ap())
    gnn_kernel(nc, *args)
    r = _run(nc, [arrays], core_ids=[0])
    return r.results[0]["out_0_dram"]
```

```python
import math
from contextlib import ExitStack

import concourse.bass as bass
from concourse import mybir

F32 = mybir.dt.float32
I32 = mybir.dt.int32
BF16 = mybir.dt.bfloat16
ALU = mybir.AluOpType
ACT = mybir.ActivationFunctionType

P = 128
N_NODES = 50000
N_EDGES = 25000
D = 512
C = 128
N_RBF = 20
EPS = 1e-5
LOG2 = math.log(2.0)
Y0 = 1.0 / math.sqrt(4.0 * math.pi)
Y1_SCALE = math.sqrt(3.0 / (4.0 * math.pi))

RANK_TILES = -(-N_EDGES // P)
CHUNK = 7
N_CHUNKS = RANK_TILES // CHUNK
UNROLL = 4
UNITS = (4, 3)
LAG = 4
DIGIT = 256
HIGHS = N_NODES // DIGIT + 1
ACT_HIGHS = (1, 3, 5)
HIGH_SLOTS = 3
PAD_KEY = HIGHS * DIGIT - 1
ATTR = 4 + N_RBF
REC = 32
W_NODE, W_SOURCE, W_WEIGHT, W_VEC, W_RBF = 0, 1, 2, 3, 6

GROUP = 4
REAL = P - 1
N_GROUPS = -(-N_EDGES // (GROUP * REAL))
SORTED = RANK_TILES * P
PAD_ROWS = 11
N_ROWS = 1 + SORTED + PAD_ROWS * P
SKIP = 65536.0
SLOTS = 4
assert RANK_TILES % CHUNK == 0 and N_CHUNKS % UNROLL == 0 and N_GROUPS % SLOTS == 2
assert N_ROWS > GROUP * REAL * (N_GROUPS + 2) + 1

COPY_CHUNKS = 100
COPY_FIRST = 22
COPY_PER_CHUNK = 3


def at_least(eng, sem, value):
    if not (isinstance(value, int) and value <= 0):
        eng.wait_ge(sem, value)


def wait_apart(eng, sem, value, passed):
    eng.wait_ge(sem, value)
    eng.sem_inc(passed, 1)


def gnn_kernel(nc, x, src_cols, src_rows, dst_cols, attrs, w_in_s, w_in_v, wf1, bf1, wf2, bf2,
               w1_s, w1_v, w2_s, w2_v, out):
    table = nc.dram_tensor("records_by_node", [N_ROWS, REC], F32, kind="Internal").ap()

    ctx = ExitStack()
    with ctx:
        def sb(name, shape, dt=F32):
            return ctx.enter_context(nc.sbuf_tensor(name, shape, dt))

        def sem(name):
            return ctx.enter_context(nc.semaphore(name))

        ident = sb("ident", [P, P])
        ones_m = sb("ones_m", [P, P])
        after = sb("after", [P, P])
        before = sb("before", [P, UNITS[0] * P])
        iota_f = sb("iota_f", [P, DIGIT])
        iota_b = sb("iota_b", [P, DIGIT], BF16)
        iota_p = sb("iota_p", [P, 2])
        zeros_b = sb("zeros_b", [P, DIGIT], BF16)

        prod_room = sb("prod_room", [P, 2 * 6 * GROUP * P])
        y_room = sb("y_room", [P, 2 * GROUP * D])
        prod = prod_room[:].rearrange("p (s n e) -> p s n e", s=2, n=6)
        y = y_room[:].rearrange("p (s g d) -> p s g d", s=2, g=GROUP)

        def part(room, start, *dims, dt=F32):
            per = 2 if dt == BF16 else 1
            flat = room[:, start:start + math.prod(dims) // per]
            if dt != F32:
                flat = flat.bitcast(dt)
            if len(dims) == 1:
                return flat
            names = "abcd"[:len(dims)]
            return flat.rearrange(f"p ({' '.join(names)}) -> p {' '.join(names)}", **dict(zip(names, dims)))

        TILE_KEYS = CHUNK * P
        onehot_t = part(prod_room, 0, 2, 2, TILE_KEYS, dt=BF16)
        keyrow = part(prod_room, 2 * TILE_KEYS, 2, TILE_KEYS, dt=I32)
        junk_same = part(prod_room, 4 * TILE_KEYS, 2, UNITS[0] * P, dt=BF16)
        onehot = part(prod_room, 4 * TILE_KEYS + UNITS[0] * P, CHUNK, 2, DIGIT, dt=BF16)
        assert 4 * TILE_KEYS + UNITS[0] * P + CHUNK * DIGIT <= 2 * 6 * GROUP * P
        count, upto, base = (part(y_room, n * 2 * DIGIT, 2, DIGIT) for n in range(3))
        counts_sb = part(y_room, 6 * DIGIT, 2, 2, 2, DIGIT, dt=BF16)
        junk_look = part(y_room, 10 * DIGIT, 2, DIGIT)
        hirow = part(y_room, 12 * DIGIT, TILE_KEYS, dt=I32)
        assert 12 * DIGIT + TILE_KEYS <= 2 * GROUP * D

        key_i = sb("key_i", [P, RANK_TILES], I32)
        dst_i = sb("dst_i", [P, RANK_TILES], I32)
        digit_i = sb("digit_i", [P, 2, RANK_TILES], I32)
        digits = sb("digits", [P, 4, RANK_TILES + CHUNK])
        dig = sb("dig", [P, UNROLL, 4, CHUNK])
        minus_p = sb("minus_p", [P, 1])
        high_far = sb("high_far", [P, HIGH_SLOTS + 1, HIGHS], BF16)
        high_far_t = sb("high_far_t", [P, CHUNK * P], BF16)
        row_total = sb("row_total", [P, 2])
        row_base = sb("row_base", [P, 2])
        looked = sb("looked", [P, 2, CHUNK])
        same = sb("same", [P, 2, CHUNK])
        place = sb("place", [P, CHUNK])
        place_i = sb("place_i", [P, UNROLL, CHUNK], I32)
        recs = sb("recs", [P, UNROLL, CHUNK, REC])
        padrec = sb("padrec", [P, PAD_ROWS, REC])

        wraw = sb("wraw", [P, 8, C])
        wf2_raw = sb("wf2_raw", [P, 4 * C])
        w_t = sb("w_t", [P, 2, C])
        wf1_sb = sb("wf1_sb", [N_RBF, C])
        bf1_sb = sb("bf1_sb", [P, 1])
        bf2_sb = sb("bf2_sb", [P, 4])
        wf2_sb = sb("wf2_sb", [P, 4, C])
        w_a, w_b, m_a, m_b, u_c, u_d, w2_sb = (
            sb(n, [P, C]) for n in ("w_a", "w_b", "m_a", "m_b", "u_c", "u_d", "w2_sb"))

        rec = sb("rec", [P, SLOTS, GROUP, REC + 1])
        scat_i = sb("scat_i", [P, SLOTS, GROUP], I32)
        xg = sb("xg", [P, SLOTS, GROUP, D])
        xs = sb("xs", [P, SLOTS, GROUP, D])
        stats = sb("stats", [P, GROUP, 6])
        mv = sb("mv", [P, GROUP, 2])
        sq = sb("sq", [P, GROUP, 3])
        sq_sum = sb("sq_sum", [P, GROUP])
        idx_f = sb("idx_f", [P, 3, GROUP])
        var = sb("var", [P, 8])
        rsq = sb("rsq", [P, 2, 8])
        newt = sb("newt", [P, 4, 8])
        scale = sb("scale", [P, 2, GROUP])
        unit = sb("unit", [P, SLOTS, GROUP, 3])
        gsum = sb("gsum", [P, 2, 3, GROUP, C])
        sel = sb("sel", [P, 2, GROUP, P])
        ft_sb = sb("ft_sb", [N_RBF, GROUP * P])
        fa = sb("fa", [P, 3, GROUP * P])
        fr = sb("fr", [P, GROUP * P])
        sp_t = sb("sp_t", [P, GROUP * P])
        sp_m = sb("sp_m", [P, GROUP * P])
        h_t = sb("h_t", [P, 5, GROUP * P])
        w_sb = sb("w_sb", [P, 4, GROUP * P])
        zq = sb("zq", [P, 2, C])
        s_sb = sb("s_sb", [P, GROUP, C])
        ba = sb("ba", [P, 3, GROUP * P])
        br = sb("br", [P, GROUP * P])
        ssp_t = sb("ssp_t", [P, GROUP * P])

        psum = [ctx.enter_context(nc.psum_tensor(f"bank{i}", [P, 512], F32)) for i in range(8)]
        FB = psum[0:4]
        b_sq, b_z, b_seg, b_s = psum[4:8]
        counts_ps, off_ps, look_ps = psum[0], psum[1], psum[2:6]

        S = {}
        for n in """keys_in iotas consts digits_made dig_made onehots_free onehots_made counts_upper counts_split
                    totals_made offsets_made base_made counts_moved onehot_t_made looked_up look_free high_far_made high_made high_t_far high_t_made
                    same_made hist_step place_summed places_made pads_made pads_out
                    weights_in weights_t weights_tc weights_u weights_made copied
                    idx_made squares rsq_made newton scale_made unit_made
                    stats_made mv_made var_made h_made g_first g_part pre_made
                    keyb_ready ft_ready h1_ready t_ready j_ready w_ready sq_ready z_ready seg_ready st_ready s2_ready
                    ft_copied h1_read f_exp f_ln t_copied w_copied sq_copied s_copied st_read b_exp b_ln
                    sel_made sel_done sp_done prod_done y_made v_added ssp_done s_added zeroed pool_passed dve_passed carried carry_start f_abs b_abs ys_made hirow_made""".split():
            S[n] = sem(n)
        chunk_keys = [sem(f"chunk_keys{h}") for h in range(2)]
        chunk_recs = [sem(f"chunk_recs{h}") for h in range(UNROLL)]
        chunk_out = [sem(f"chunk_out{h}") for h in range(UNROLL)]
        rec_in = [sem(f"rec_in{k}") for k in range(SLOTS)]
        xg_in = [sem(f"xg_in{k}") for k in range(SLOTS)]
        xs_in = [sem(f"xs_in{k}") for k in range(SLOTS)]
        rows_out = [sem(f"rows_out{k}") for k in range(SLOTS)]
        SORT_LOOPS = N_CHUNKS // UNROLL
        N_LOOPS = N_GROUPS // SLOTS

        def steps(eng, step, first):
            for s in range(first, SLOTS):
                step(s, s // SLOTS, s % SLOTS)
            with eng.Fori(1, N_LOOPS) as i:
                for k in range(SLOTS):
                    step(SLOTS * i + k, i, k)
            for s in range(SLOTS * N_LOOPS, N_GROUPS):
                step(s, N_LOOPS, s % SLOTS)

        def loads(i, k, ahead, per):
            return per * 16 * (i + (k + ahead) // SLOTS + 1)

        block = ctx.enter_context(nc.Block())

        @block.sync
        def _(sp):
            sp.dma_start(key_i[:], src_cols).then_inc(S["keys_in"], 16)
            sp.dma_start(dst_i[:], dst_cols).then_inc(S["keys_in"], 16)
            for n, w in enumerate((w_in_s, w_in_v, w1_s[0:2 * C:2, :], w1_s[1:2 * C:2, :],
                                   w1_v[0:2 * C:2, :], w1_v[1:2 * C:2, :], w2_s, w2_v)):
                sp.dma_start(wraw[:, n, :], w).then_inc(S["weights_in"], 16)
            sp.dma_start(wf2_raw[:], wf2[:, 0:4 * C]).then_inc(S["weights_in"], 16)
            sp.dma_start(wf1_sb[:], wf1).then_inc(S["weights_in"], 16)
            sp.dma_start(bf1_sb[:], bf1.rearrange("(c a) -> c a", a=1)).then_inc(S["weights_in"], 16)
            for v in range(2):
                sp.dma_start(bf2_sb[:, 2 * v:2 * v + 2],
                             bf2[2 * C * v:2 * C * (v + 1)].rearrange("(c a) -> c a", a=2)).then_inc(S["weights_in"], 16)
            rows = src_rows.rearrange("(a n) -> a n", a=1)
            attr = attrs.rearrange("p (t w) -> p t w", w=ATTR)
            sp.wait_ge(S["consts"], 2)

            def load_keys(c, h):
                sp.dma_start(keyrow[:, h, :], rows[:, bass.ds(c * TILE_KEYS, TILE_KEYS)].to_broadcast([P, TILE_KEYS])).then_inc(chunk_keys[h], 16)

            def load_recs(c, hh):
                sp.dma_start(recs[:, hh, :, 2:2 + ATTR], attr[:, bass.ds(c * CHUNK, CHUNK), :]).then_inc(chunk_recs[hh], 16)

            for hh in range(UNROLL):
                if hh < 2:
                    load_keys(hh, hh)
                load_recs(hh, hh)
            per = N_NODES // 5 // COPY_CHUNKS
            x5 = x.rearrange("(a b) c -> a (b c)", b=5)
            o5 = out.rearrange("(a b) c -> a (b c)", b=5)

            def copy(c):
                sp.dma_start(o5[bass.ds(c * per, per), :], x5[bass.ds(c * per, per), :]).then_inc(S["copied"], 16)

            for c in range(COPY_FIRST):
                copy(c)

            def next_keys(c, hh):
                sp.wait_ge(S["same_made"], (c - 1) * CHUNK + 2)
                load_keys(c, hh % 2)
                for n in range(COPY_PER_CHUNK):
                    copy(c * COPY_PER_CHUNK + (COPY_FIRST + n - 2 * COPY_PER_CHUNK))

            for c in range(2, UNROLL):
                next_keys(c, c)
            with sp.Fori(1, SORT_LOOPS) as i:
                for hh in range(UNROLL):
                    sp.wait_ge(chunk_out[hh], i * (16 * CHUNK))
                    load_recs(UNROLL * i + hh, hh)
                    next_keys(UNROLL * i + hh, hh)
            for c in range(COPY_FIRST + (N_CHUNKS - 2) * COPY_PER_CHUNK, COPY_CHUNKS):
                copy(c)
            sp.wait_ge(S["pads_made"], 3)
            sp.dma_start(table[0:1, :], padrec[0:1, 0, :]).then_inc(S["pads_out"], 16)
            sp.dma_start(table[1 + SORTED:N_ROWS, :].rearrange("(p a) w -> p a w", a=PAD_ROWS), padrec[:]).then_inc(S["pads_out"], 16)
            sp.wait_ge(S["pads_out"], 32)
            for hh in range(UNROLL):
                sp.wait_ge(chunk_out[hh], 16 * CHUNK * SORT_LOOPS)

            def load_rec(g, slot):
                src = bass.AP(table.tensor, g * (GROUP * REAL * REC), [[REC, P], [REAL * REC, GROUP], [1, REC + 1]])
                sp.dma_start(rec[:, slot, :, :], src).then_inc(rec_in[slot], 16)

            for g in range(SLOTS):
                load_rec(g, g)
            with sp.Fori(0, N_LOOPS) as i:
                for k in range(SLOTS):
                    s = SLOTS * i + k
                    sp.wait_ge(S["sel_done"], s + 1)
                    sp.wait_ge(S["ft_ready"], s + 1)
                    sp.wait_ge(S["scale_made"], 2 * s + 2)
                    load_rec(s + SLOTS, k)
            for k in range(SLOTS):
                sp.wait_ge(rows_out[k], 16 * GROUP * len(range(k, N_GROUPS, SLOTS)))
            for k in range(2):
                sp.wait_ge(rec_in[(N_GROUPS + k) % SLOTS], 16 * (N_LOOPS + 1))

        @block.gpsimd
        def _(g):
            pool = nc.gpsimd
            pool.iota(iota_f[:], [[1, DIGIT]], base=0, channel_multiplier=0, allow_small_or_imprecise_dtypes=True).then_inc(S["iotas"], 1)
            pool.iota(iota_p[:], [[P, 2]], base=0, channel_multiplier=1, allow_small_or_imprecise_dtypes=True).then_inc(S["iotas"], 1)
            pool.memset(ones_m[:], 1.0).then_inc(S["consts"], 1)
            pool.memset(recs[:], 0.0).then_inc(S["consts"], 1)
            pool.memset(zeros_b[:], 0.0).then_inc(S["consts"], 1)
            g.wait_ge(S["consts"], 3)
            for m, sign, op in ((ident[:], 1, ALU.is_equal), (after[:], -1, ALU.is_gt), (before[:, (UNITS[0] - 1) * P:UNITS[0] * P], 1, ALU.is_gt)):
                pool.affine_select(out=m, in_=ones_m[:], compare_op=op, fill=0.0, base=0,
                                   pattern=[[-sign, P]], channel_multiplier=sign).then_inc(S["consts"], 1)
            pool.memset(before[:, 0:(UNITS[0] - 1) * P], 1.0).then_inc(S["consts"], 1)
            pool.memset(padrec[:], 1.0).then_inc(S["pads_made"], 1)
            g.wait_ge(S["pads_made"], 1)
            pool.memset(padrec[:, :, W_NODE], float(PAD_KEY)).then_inc(S["pads_made"], 1)
            pool.memset(padrec[:, :, W_SOURCE].bitcast(I32), 0).then_inc(S["pads_made"], 1)
            pool.memset(xs[:], 0.0).then_inc(S["zeroed"], 1)
            pool.memset(var[:], 1.0).then_inc(S["zeroed"], 1)
            last_row = g.to_reg(N_ROWS - 1)
            last_node = g.to_reg(N_NODES - 1)
            with g.Fori(0, SORT_LOOPS) as i:
                for hh in range(UNROLL):
                    c = UNROLL * i + hh
                    g.wait_ge(S["places_made"], c + 1)
                    g.sem_inc(S["pool_passed"], 1)
                    for j in range(CHUNK):
                        pool.indirect_dma_start(table, bass.IndirectOffsetOnAxis(ap=place_i[:, hh, j:j + 1], axis=0),
                                                recs[:, hh, j, :], None, bounds_check=last_row, oob_is_err=False).then_inc(chunk_out[hh], 16)

            def step(s, i, k):
                q = (k + 3) % SLOTS
                n = s + 3
                if n < N_GROUPS + 1 if isinstance(n, int) else True:
                    g.wait_ge(rec_in[q], loads(i, k, 3, 1))
                    at_least(g, rows_out[q], loads(i, k, -1, GROUP))
                    node, following = rec[:, q, :, W_NODE], rec[:, q, :, REC]
                    pool.tensor_tensor(idx_f[:, 0, :], following, node, ALU.subtract).then_inc(S["idx_made"], 1)
                    wait_apart(g, S["idx_made"], 5 * n + 1, S["pool_passed"])
                    pool.tensor_scalar(idx_f[:, 1, :], idx_f[:, 0, :], 1.0, -SKIP, ALU.min, ALU.mult).then_inc(S["idx_made"], 1)
                    g.wait_ge(S["idx_made"], 5 * n + 2)
                    pool.tensor_tensor(idx_f[:, 2, :], idx_f[:, 1, :], node, ALU.add).then_inc(S["idx_made"], 1)
                    wait_apart(g, S["idx_made"], 5 * n + 3, S["pool_passed"])
                    pool.tensor_scalar(scat_i[:, q, :], idx_f[:, 2, :], SKIP, None, ALU.add).then_inc(S["idx_made"], 1)
                    wait_apart(g, S["idx_made"], 5 * n + 4, S["pool_passed"])
                    pool.memset(scat_i[0:1, q, :], int(SKIP)).then_inc(S["idx_made"], 1)
                    vec = rec[:, q, :, W_VEC:W_VEC + 3]
                    at_least(g, S["rsq_made"], 2 * n)
                    pool.tensor_tensor(sq[:], vec, vec, ALU.mult).then_inc(S["squares"], 1)
                    g.wait_ge(S["squares"], 3 * n + 1)
                    pool.tensor_tensor(sq_sum[:], sq[:, :, 0], sq[:, :, 1], ALU.add).then_inc(S["squares"], 1)
                    g.wait_ge(S["squares"], 3 * n + 2)
                    at_least(g, S["newton"], 4 * n)
                    pool.tensor_tensor(var[:, 4:8], sq_sum[:], sq[:, :, 2], ALU.add).then_inc(S["squares"], 1)
                    at_least(g, S["t_ready"], 5 * s)
                    g.sem_inc(S["pool_passed"], 1)
                    for j in range(GROUP):
                        pool.indirect_dma_start(xg[:, q, j, :], None, x,
                                                bass.IndirectOffsetOnAxis(ap=rec[:, q, j, W_SOURCE:W_SOURCE + 1].bitcast(I32), axis=0),
                                                bounds_check=last_node, oob_is_err=False).then_inc(xg_in[q], 16)
                p = s + 2
                if not isinstance(p, int) or 0 <= p < N_GROUPS:
                    z = (k + 2) % SLOTS
                    at_least(g, rows_out[z], loads(i, k, -2, GROUP))
                    at_least(g, S["idx_made"], 5 * p + 5)
                    g.sem_inc(S["pool_passed"], 1)
                    for j in range(GROUP):
                        pool.indirect_dma_start(xs[:, z, j, :], None, x,
                                                bass.IndirectOffsetOnAxis(ap=scat_i[:, z, j:j + 1], axis=0),
                                                bounds_check=last_node, oob_is_err=False).then_inc(xs_in[z], 16)
                if not isinstance(p, int) or p < N_GROUPS:
                    g.wait_ge(S["rsq_made"], 2 * n + 2)
                    pool.tensor_tensor(newt[:, 0, :], rsq[:, 1, :], rsq[:, 1, :], ALU.mult).then_inc(S["newton"], 1)
                    g.wait_ge(S["newton"], 4 * n + 1)
                    pool.tensor_tensor(newt[:, 1, :], newt[:, 0, :], var[:], ALU.mult).then_inc(S["newton"], 1)
                    wait_apart(g, S["newton"], 4 * n + 2, S["pool_passed"])
                    pool.tensor_scalar(newt[:, 2, :], newt[:, 1, :], -0.5, 1.5, ALU.mult, ALU.add).then_inc(S["newton"], 1)
                    g.wait_ge(S["newton"], 4 * n + 3)
                    at_least(g, S["unit_made"], n)
                    pool.tensor_tensor(newt[:, 3, :], newt[:, 2, :], rsq[:, 1, :], ALU.mult).then_inc(S["newton"], 1)
                    g.wait_ge(S["newton"], 4 * n + 4)
                    at_least(g, S["y_made"], 4 * s)
                    pool.tensor_tensor(unit[:, q, :, :], rec[:, q, :, W_VEC:W_VEC + 3],
                                       newt[:, 3, 4:8].rearrange("p (g a) -> p g a", a=1).to_broadcast([P, GROUP, 3]),
                                       ALU.mult).then_inc(S["unit_made"], 1)
                    if not isinstance(p, int) or p >= 0:
                        z = (k + 2) % SLOTS
                        at_least(g, S["sel_done"], s + 1)
                        pool.tensor_tensor(scale[:, k % 2, :], newt[:, 3, 0:4], rec[:, z, :, W_WEIGHT], ALU.mult).then_inc(S["scale_made"], 1)
                        wait_apart(g, S["scale_made"], 2 * p + 1, S["pool_passed"])
                        pool.memset(scale[0:1, k % 2, :], 1.0).then_inc(S["scale_made"], 1)
                if not isinstance(s, int) or s >= 0:
                    g.wait_ge(S["s_added"], s + 1)
                    g.wait_ge(S["copied"], 16 * COPY_CHUNKS)
                    g.sem_inc(S["pool_passed"], 1)
                    for j in range(GROUP):
                        pool.indirect_dma_start(out, bass.IndirectOffsetOnAxis(ap=scat_i[:, k, j:j + 1], axis=0),
                                                xs[:, k, j, :], None, bounds_check=last_node, oob_is_err=False).then_inc(rows_out[k], 16)

            g.wait_ge(S["zeroed"], 2)
            steps(g, step, -3)
            g.wait_ge(xg_in[N_GROUPS % SLOTS], 16 * GROUP * (N_LOOPS + 1))

        @block.scalar
        def _(a):
            act = nc.scalar.activation
            root = 1.0 / math.sqrt(C)
            mix = 1.0 / math.sqrt(2 * C)
            nc.scalar.preload_act_table_set("natural_log_exp_and_others")
            a.sem_inc(S["high_made"], HIGH_SLOTS)

            def highs(tiles, slots, hh, n, free=None):
                for m, (j, slot) in enumerate(zip(tiles, slots)):
                    a.wait_ge(S["high_made"], n + m + 1)
                    act(high_far[:, slot, :], iota_b[:, 0:HIGHS], ACT.Abs, bias=dig[:, hh, 3, j:j + 1]).then_inc(S["high_far_made"], 1)
                for m, (j, slot) in enumerate(zip(tiles, slots)):
                    if free is not None:
                        a.wait_ge(S["onehots_free"], free + j + 1)
                    a.wait_ge(S["high_far_made"], n + m + 1)
                    act(onehot[:, j, 0, 0:HIGHS], high_far[:, slot, :], ACT.Relu, scale=-1.0, bias=1.0).then_inc(S["high_made"], 1)

            with a.Fori(0, SORT_LOOPS) as i:
                for hh in range(UNROLL):
                    c = UNROLL * i + hh
                    a.wait_ge(S["dig_made"], c + 1)
                    highs(ACT_HIGHS, range(HIGH_SLOTS), hh, c * len(ACT_HIGHS), free=c * CHUNK)

            a.wait_ge(S["weights_in"], 16 * 13)
            a.wait_ge(S["weights_t"], 1)
            act(w_t[:], b_sq[:, 0:2 * C].rearrange("p (a c) -> p a c", a=2), ACT.Copy).then_inc(S["weights_tc"], 1)
            for n, (dst, src, factor) in enumerate((
                    (w_a, wraw[:, 0, :], root), (w_b, wraw[:, 1, :], root),
                    (m_a, wraw[:, 2, :], mix * Y0), (m_b, wraw[:, 3, :], mix * Y1_SCALE / math.sqrt(3.0)),
                    (w2_sb, wraw[:, 6, :], root))):
                act(dst[:], src, ACT.Copy, scale=factor).then_inc(S["weights_made"], 1)
            for v in range(2):
                for b in range(2):
                    cols = wf2_raw[:, 2 * C * v:2 * C * (v + 1)].rearrange("p (c a) -> p a c", a=2)[:, b, :]
                    act(wf2_sb[:, 2 * v + b, :], cols, ACT.Copy).then_inc(S["weights_made"], 1)
            a.wait_ge(S["weights_u"], 1)
            act(u_c[:], b_z[:, 0:C], ACT.Copy, scale=mix * root * Y1_SCALE).then_inc(S["weights_made"], 1)
            act(u_d[:], b_z[:, C:2 * C], ACT.Copy, scale=mix * root * Y0).then_inc(S["weights_made"], 1)

            def upper_counts(c, e):
                a.wait_ge(S["counts_moved"], 2 * c + e + 1)
                a.wait_ge(S["looked_up"], c * CHUNK + (UNITS[0] - UNITS[1] if e == 0 else UNITS[0]))
                act(counts_sb[:, e, 0, :, :], counts_ps[:].rearrange("p (a b) -> p a b", a=2), ACT.Copy).then_inc(S["counts_upper"], 1)

            def chunks(i, first=False):
                for hh in range(UNROLL):
                    c = UNROLL * i + hh
                    h = hh % 2
                    n = N_CHUNKS * len(ACT_HIGHS) + c * CHUNK
                    a.wait_ge(S["dig_made"], N_CHUNKS + c + 1)
                    if not (first and hh == 0):
                        a.wait_ge(S["counts_moved"], 2 * c)
                    highs((0, 1), (0, 1), hh, n)
                    upper_counts(c, 0)
                    highs((2, 3), (2, 3), hh, n + 2)
                    a.wait_ge(S["hirow_made"], c + 1)
                    at_least(a, S["high_t_made"], c)
                    act(high_far_t[:], hirow, ACT.Abs, bias=minus_p[:]).then_inc(S["high_t_far"], 1)
                    if not (first and hh == 0):
                        a.wait_ge(S["counts_moved"], 2 * c + 1)
                    highs((4, 5), (0, 1), hh, n + 4)
                    a.wait_ge(S["high_t_far"], c + 1)
                    act(onehot_t[:, h, 0, :], high_far_t[:], ACT.Relu, scale=-1.0, bias=1.0).then_inc(S["high_t_made"], 1)
                    upper_counts(c, 1)
                    highs((6,), (2,), hh, n + 6)

            chunks(0, first=True)
            with a.Fori(1, SORT_LOOPS) as i:
                chunks(i)

            def t_copy(f, i):
                a.wait_ge(S["t_ready"], 5 * f + i + 1)
                at_least(a, S["j_ready"], 5 * f)
                act(h_t[:, i, :], FB[(3 + i) % 4][:], ACT.Copy).then_inc(S["t_copied"], 1)

            def w_copy(f, i):
                bank, bias = ((0, 0), (1, 2), (3, 1), (1, 3))[i]
                a.wait_ge(S["w_ready"], 4 * f + i + 1)
                at_least(a, S["prod_done"], 6 * f)
                act(w_sb[:, i, :], FB[bank][:], ACT.Identity, bias=bf2_sb[:, bias:bias + 1]).then_inc(S["w_copied"], 1)

            def sq_copy(b, k, j):
                a.wait_ge(S["sq_ready"], 4 * b + j + 1)
                act(y[:, k % 2, j, 0:C], b_sq[:, 0:C], ACT.Copy).then_inc(S["ys_made"], 1)
                act(zq[:, j % 2, :], b_sq[:, C:2 * C], ACT.Copy).then_inc(S["sq_copied"], 1)

            def s_copy(b, j):
                a.wait_ge(S["seg_ready"], 4 * b + j + 1)
                at_least(a, S["st_ready"], b)
                act(s_sb[:, j, :], b_seg[:, 0:C], ACT.Copy).then_inc(S["s_copied"], 1)

            def carry(t, par, j):
                a.wait_ge(S["v_added"], t + 1)
                a.wait_ge(S["y_made"], t + 2)
                a.wait_ge(S["ys_made"], t + 2)
                act(y[0:1, par, j, :], b_seg[0:1, :], ACT.Copy).then_inc(S["carried"], 1)

            def step(s, i, k):
                b, f, n = s, s + 1, s + 3
                known = isinstance(s, int)
                back, front, pre = (not known or s >= 0), (not known or 0 <= s + 1 < N_GROUPS), (not known or s + 2 < N_GROUPS)
                if front:
                    a.wait_ge(S["ft_ready"], f + 1)
                    at_least(a, S["h1_ready"], f)
                    act(ft_sb[:], FB[1][0:N_RBF, :], ACT.Copy).then_inc(S["ft_copied"], 1)
                if back:
                    sq_copy(b, k, 0)
                    carry(4 * b - 1, k % 2, 0)
                if front:
                    a.wait_ge(S["h1_ready"], f + 1)
                    at_least(a, S["f_exp"], f)
                    act(fa[:, 0, :], FB[2][:], ACT.Abs, bias=bf1_sb[:]).then_inc(S["f_abs"], 1)
                if back:
                    sq_copy(b, k, 1)
                if front:
                    at_least(a, S["sp_done"], f)
                    act(fr[:], FB[2][:], ACT.Relu, bias=bf1_sb[:]).then_inc(S["h1_read"], 1)
                    a.wait_ge(S["f_abs"], f + 1)
                    at_least(a, S["f_ln"], f)
                    act(fa[:, 1, :], fa[:, 0, :], ACT.Exp, scale=-1.0).then_inc(S["f_exp"], 1)
                if back:
                    s_copy(b, 0)
                if front:
                    t_copy(f, 0)
                    a.wait_ge(S["f_exp"], f + 1)
                    act(fa[:, 2, :], fa[:, 1, :], ACT.Ln, bias=1.0).then_inc(S["f_ln"], 1)
                if back:
                    carry(4 * b, k % 2, 1)
                if front:
                    t_copy(f, 1)
                    t_copy(f, 2)
                if back:
                    sq_copy(b, k, 2)
                    s_copy(b, 1)
                    carry(4 * b + 1, k % 2, 2)
                if front:
                    t_copy(f, 3)
                    t_copy(f, 4)
                if front:
                    w_copy(f, 0)
                if back:
                    sq_copy(b, k, 3)
                if pre:
                    at_least(a, S["var_made"], s + 3)
                    a.wait_ge(S["squares"], 3 * n + 3)
                    at_least(a, S["rsq_made"], 2 * n)
                    act(rsq[:, 0, :], var[:], ACT.Ln).then_inc(S["rsq_made"], 1)
                    a.wait_ge(S["rsq_made"], 2 * n + 1)
                    at_least(a, S["newton"], 4 * n)
                    act(rsq[:, 1, :], rsq[:, 0, :], ACT.Exp, scale=-0.5).then_inc(S["rsq_made"], 1)
                if front:
                    w_copy(f, 1)
                if back:
                    s_copy(b, 2)
                    carry(4 * b + 2, k % 2, 3)
                if front:
                    w_copy(f, 2)
                if back:
                    s_copy(b, 3)
                    a.wait_ge(S["st_ready"], b + 1)
                    at_least(a, S["b_exp"], b)
                    act(ba[:, 0, :], b_s[:], ACT.Abs).then_inc(S["b_abs"], 1)
                    at_least(a, S["ssp_done"], b)
                    act(br[:], b_s[:], ACT.Relu).then_inc(S["st_read"], 1)
                if front:
                    w_copy(f, 3)
                if back:
                    a.wait_ge(S["b_abs"], b + 1)
                    at_least(a, S["b_ln"], b)
                    act(ba[:, 1, :], ba[:, 0, :], ACT.Exp, scale=-1.0).then_inc(S["b_exp"], 1)
                    a.wait_ge(S["b_exp"], b + 1)
                    act(ba[:, 2, :], ba[:, 1, :], ACT.Ln, bias=1.0).then_inc(S["b_ln"], 1)

            a.wait_ge(S["zeroed"], 2)
            a.wait_ge(S["carry_start"], 1)
            steps(a, step, -3)

        @block.tensor
        def _(pe):
            mm, tr = nc.tensor.matmul, nc.tensor.transpose
            def add_counts(slot):
                for c in range(2):
                    rows = min(HIGHS - P * c, P)
                    m = mm(counts_ps[0:rows, DIGIT * c:DIGIT * (c + 1)], onehot[:, slot, 0, P * c:P * c + rows], onehot[:, slot, 1, :],
                           start=False, stop=False, skip_group_check=True)
                return m

            pe.wait_ge(S["consts"], 7)
            pe.sem_inc(S["onehots_free"], CHUNK)
            pe.sem_inc(S["looked_up"], UNITS[0])
            mm(counts_ps[:, 0:DIGIT], zeros_b[:, 0:P], zeros_b[:], start=True, stop=False, skip_group_check=True)
            mm(counts_ps[:, DIGIT:2 * DIGIT], zeros_b[:, 0:P], zeros_b[:], start=False, stop=False, skip_group_check=True)
            with pe.Fori(0, N_CHUNKS) as i:
                for k in range(CHUNK):
                    pe.wait_ge(S["onehots_made"], i * CHUNK + k + 1)
                    if k in ACT_HIGHS:
                        pe.wait_ge(S["high_made"], i * len(ACT_HIGHS) + ACT_HIGHS.index(k) + HIGH_SLOTS + 1)
                    add_counts(k).then_inc(S["onehots_free"], 1)
            pe.wait_ge(S["weights_in"], 16 * 13)
            tr(b_sq[:, 0:C], wraw[:, 4, :], ident[:])
            tr(b_sq[:, C:2 * C], wraw[:, 5, :], ident[:]).then_inc(S["weights_t"], 1)
            pe.wait_ge(S["weights_tc"], 1)
            mm(b_z[:, 0:C], w_t[:, 0, :], wraw[:, 7, :], start=True, stop=True)
            mm(b_z[:, C:2 * C], w_t[:, 1, :], wraw[:, 7, :], start=True, stop=True).then_inc(S["weights_u"], 1)
            pe.wait_ge(S["totals_made"], 1)
            mm(off_ps[:, 0:1], after[:], row_total[:, 0:1], start=True, stop=True)
            mm(off_ps[:, 1:2], after[:], row_total[:, 1:2], start=True, stop=False)
            mm(off_ps[:, 1:2], ones_m[:], row_total[:, 0:1], start=False, stop=True).then_inc(S["offsets_made"], 1)
            pe.wait_ge(S["base_made"], 1)
            mm(counts_ps[:], ident[:], base.rearrange("p a b -> p (a b)"), start=True, stop=False, skip_group_check=True).then_inc(S["counts_moved"], 1)
            with pe.Fori(0, SORT_LOOPS) as i:
                for hh in range(UNROLL):
                    for e, start in enumerate((0, UNITS[0])):
                        tiles = range(start, start + UNITS[e])
                        pe.wait_ge(S["counts_split"], 2 * (UNROLL * i + hh) + e + 1)
                        for j in tiles:
                            pe.wait_ge(S["onehots_made"], RANK_TILES + (UNROLL * i + hh) * CHUNK + j + 1)
                            pe.wait_ge(S["high_made"], N_CHUNKS * len(ACT_HIGHS) + (UNROLL * i + hh) * CHUNK + j + HIGH_SLOTS + 1)
                            m = add_counts(j)
                        m.then_inc(S["counts_moved"], 1)
                        if e == 0:
                            pe.wait_ge(S["onehot_t_made"], UNROLL * i + hh + 1)
                            pe.wait_ge(S["high_t_made"], UNROLL * i + hh + 1)
                        for j in tiles:
                            k = hh * CHUNK + j
                            pe.wait_ge(S["look_free"], i * (UNROLL * CHUNK) + k + 1)
                            for c in range(2):
                                for bits in range(2):
                                    m = mm(look_ps[k % 4][:, 0:DIGIT], onehot_t[:, hh % 2, c, j * P:(j + 1) * P], counts_sb[:, e, bits, c, :],
                                           start=(c == 0 and bits == 0), stop=(c == 1 and bits == 1))
                            m.then_inc(S["looked_up"], 1)

            tile = [slice(j * P, (j + 1) * P) for j in range(GROUP)]

            def scalars_out(b):
                pe.wait_ge(S["ssp_done"], b + 1)
                pe.wait_ge(S["st_read"], b + 1)
                for j in range(GROUP):
                    m = mm(b_s[:, tile[j]], ssp_t[:, tile[j]], w2_sb[:], start=True, stop=True)
                m.then_inc(S["s2_ready"], 1)

            def step(s, i, k):
                b, f = s, s + 1
                known = isinstance(s, int)
                back, front = (not known or s >= 0), (not known or 0 <= s + 1 < N_GROUPS)
                q = (k + 1) % SLOTS
                fp, bp = (k + 1) % 2, k % 2

                def t_item(n):
                    bank = FB[(3 + n) % 4]
                    for j in range(GROUP):
                        if n == 4:
                            src = gsum[:, fp, 2, j, :]
                        elif n == 0:
                            src = xg[:, q, j, 0:C]
                        else:
                            src = xg[:, q, j, C:D].rearrange("p (c i) -> p i c", i=3)[:, n - 1, :]
                        m = tr(bank[:, tile[j]], src, ident[:])
                    m.then_inc(S["t_ready"], 1)

                def w_item(n):
                    bank, col = ((0, 0), (1, 2), (3, 1), (1, 3))[n]
                    mm(FB[bank][:], wf2_sb[:, col, :], sp_t[:], start=True, stop=True).then_inc(S["w_ready"], 1)

                def j_item(bank, w, n):
                    mm(FB[bank][:], w[:], h_t[:, n, :], start=True, stop=True).then_inc(S["j_ready"], 1)

                def scalar_messages(j):
                    at_least(pe, S["sq_copied"], 4 * b + j)
                    mm(b_sq[:, 0:C], prod[:, bp, 0, tile[j]], m_a[:], start=True, stop=False)
                    mm(b_sq[:, 0:C], prod[:, bp, 2, tile[j]], m_b[:], start=False, stop=True)
                    mm(b_sq[:, C:2 * C], prod[:, bp, 1, tile[j]], u_c[:], start=True, stop=True).then_inc(S["sq_ready"], 1)

                def vector_messages(j):
                    at_least(pe, S["y_made"], 4 * b + j)
                    for c in range(3):
                        m = mm(b_z[:, c * C:(c + 1) * C], prod[:, bp, 3 + c, tile[j]], u_d[:], start=True, stop=True)
                    m.then_inc(S["z_ready"], 1)

                def segment(j):
                    pe.wait_ge(S["y_made"], 4 * b + j + 1)
                    pe.wait_ge(S["carried"], 4 * b + j + 1)
                    mm(b_seg[:], sel[:, bp, j, :], y[:, bp, j, :], start=True, stop=True).then_inc(S["seg_ready"], 1)

                if front:
                    pe.wait_ge(rec_in[q], loads(i, k, 1, 1))
                    at_least(pe, S["w_copied"], 4 * f)
                    for j in range(GROUP):
                        m = tr(FB[1][0:N_RBF, tile[j]], rec[:, q, j, W_RBF:W_RBF + N_RBF], ident[:])
                    m.then_inc(S["ft_ready"], 1)
                if not known or s >= 1:
                    scalars_out(b - 1)
                if front:
                    at_least(pe, S["prod_done"], 6 * f)
                    for j in range(GROUP):
                        m = tr(FB[0][:, tile[j]], rec[:, q, j, W_NODE:W_NODE + 1].to_broadcast([P, P]), ident[:])
                    m.then_inc(S["keyb_ready"], 1)
                if back:
                    pe.wait_ge(S["prod_done"], 6 * b + 6)
                    scalar_messages(0)
                    vector_messages(0)
                if front:
                    pe.wait_ge(S["ft_copied"], f + 1)
                    mm(FB[2][:], wf1_sb[:], ft_sb[:], start=True, stop=True).then_inc(S["h1_ready"], 1)
                if back:
                    scalar_messages(1)
                if front:
                    pe.wait_ge(S["pre_made"], 4 * f + 4)
                    t_item(0)
                if back:
                    vector_messages(1)
                    pe.wait_ge(S["sel_done"], b + 1)
                    segment(0)
                if front:
                    pe.wait_ge(S["sel_made"], 4 * f + 4)
                    t_item(1)
                    pe.wait_ge(S["ft_copied"], f + 1)
                    t_item(2)
                if back:
                    scalar_messages(2)
                    vector_messages(2)
                    segment(1)
                if front:
                    pe.wait_ge(S["h1_read"], f + 1)
                    t_item(3)
                    pe.wait_ge(S["t_copied"], 5 * f + 1)
                    t_item(4)
                    pe.wait_ge(S["sp_done"], f + 1)
                    pe.wait_ge(S["t_copied"], 5 * f + 2)
                    w_item(0)
                if back:
                    scalar_messages(3)
                    vector_messages(3)
                if front:
                    pe.wait_ge(S["t_copied"], 5 * f + 3)
                    w_item(1)
                if back:
                    segment(2)
                if front:
                    pe.wait_ge(S["t_copied"], 5 * f + 4)
                    j_item(2, w_a, 0)
                    pe.wait_ge(S["t_copied"], 5 * f + 5)
                    w_item(2)
                    pe.wait_ge(S["w_copied"], 4 * f + 1)
                    j_item(0, w_b, 4)
                if back:
                    segment(3)
                    pe.wait_ge(S["s_copied"], 4 * b + 4)
                    at_least(pe, S["s_added"], b)
                    for j in range(GROUP):
                        m = tr(b_s[:, tile[j]], s_sb[:, j, :], ident[:])
                    m.then_inc(S["st_ready"], 1)
                if front:
                    pe.wait_ge(S["w_copied"], 4 * f + 2)
                    w_item(3)
                    pe.wait_ge(S["prod_done"], 6 * f + 2)
                    j_item(2, w_b, 1)
                    pe.wait_ge(S["w_copied"], 4 * f + 3)
                    j_item(3, w_b, 2)
                    pe.wait_ge(S["prod_done"], 6 * f + 3)
                    j_item(0, w_b, 3)

            pe.wait_ge(S["weights_made"], 11)
            mm(b_seg[:, 0:DIGIT], zeros_b[:, 0:P], zeros_b[:], start=True, stop=True)
            mm(b_seg[:, DIGIT:2 * DIGIT], zeros_b[:, 0:P], zeros_b[:], start=True, stop=True).then_inc(S["carry_start"], 1)
            steps(pe, step, -1)
            scalars_out(N_GROUPS - 1)

        @block.vector
        def _(d):
            v = nc.vector
            d.sem_inc(S["look_free"], len(look_ps))
            d.sem_inc(S["same_made"], 2)
            d.wait_ge(S["keys_in"], 32)
            v.tensor_single_scalar(digit_i[:, 0, :], key_i[:], 8, ALU.arith_shift_right).then_inc(S["digits_made"], 1)
            v.tensor_single_scalar(digit_i[:, 1, :], key_i[:], DIGIT - 1, ALU.bitwise_and).then_inc(S["digits_made"], 1)
            d.wait_ge(S["iotas"], 2)
            v.tensor_copy(iota_b[:], iota_f[:]).then_inc(S["digits_made"], 1)
            v.tensor_copy(digits[:, 2, 0:RANK_TILES], key_i[:]).then_inc(S["digits_made"], 1)
            d.wait_ge(S["digits_made"], 4)
            v.tensor_copy(digits[:, 0:2, 0:RANK_TILES], digit_i[:]).then_inc(S["digits_made"], 1)
            v.tensor_scalar(minus_p[:], iota_p[:, 0:1], -1.0, None, ALU.mult).then_inc(S["digits_made"], 1)
            d.wait_ge(S["digits_made"], 5)
            v.tensor_scalar(digits[:, 3, 0:RANK_TILES], digits[:, 0, 0:RANK_TILES], -1.0, None, ALU.mult).then_inc(S["digits_made"], 1)
            d.wait_ge(S["digits_made"], 7)
            v.tensor_copy(digits[:, :, RANK_TILES:RANK_TILES + CHUNK], digits[:, :, 0:CHUNK]).then_inc(S["digits_made"], 1)
            v.tensor_copy(dig[:, 0, :, :], digits[:, :, 0:CHUNK]).then_inc(S["dig_made"], 1)
            d.wait_ge(S["digits_made"], 8)

            def next_digits(c, hh):
                v.tensor_copy(dig[:, (hh + 1) % UNROLL, :, :], digits[:, :, bass.ds((c + 1) * CHUNK, CHUNK)]).then_inc(S["dig_made"], 1)

            def onehots(hh, j, high):
                if high:
                    v.tensor_scalar(onehot[:, j, 0, 0:HIGHS], iota_b[:, 0:HIGHS], dig[:, hh, 0, j:j + 1], None, ALU.is_equal)
                v.tensor_scalar(onehot[:, j, 1, :], iota_b[:], dig[:, hh, 1, j:j + 1], None, ALU.is_equal).then_inc(S["onehots_made"], 1)

            with d.Fori(0, SORT_LOOPS) as i:
                for hh in range(UNROLL):
                    c = UNROLL * i + hh
                    next_digits(c, hh)
                    d.wait_ge(S["dig_made"], c + 1)
                    for j in range(CHUNK):
                        d.wait_ge(S["onehots_free"], c * CHUNK + j + 1)
                        onehots(hh, j, j not in ACT_HIGHS)
            d.wait_ge(S["onehots_free"], RANK_TILES + CHUNK)
            v.tensor_copy(count.rearrange("p a b -> p (a b)"), counts_ps[:]).then_inc(S["hist_step"], 1)
            d.wait_ge(S["hist_step"], 1)
            d.wait_ge(S["consts"], 7)
            for c in range(2):
                v.tensor_tensor_scan(upto[:, c, :], before[:, 0:DIGIT], count[:, c, :], 0.0, ALU.mult, ALU.add).then_inc(S["hist_step"], 1)
            d.wait_ge(S["hist_step"], 3)
            v.tensor_copy(row_total[:], upto[:, :, DIGIT - 1]).then_inc(S["totals_made"], 1)
            d.wait_ge(S["totals_made"], 1)
            v.tensor_tensor(upto, upto, count, ALU.subtract).then_inc(S["hist_step"], 1)
            d.wait_ge(S["offsets_made"], 1)
            v.tensor_scalar(row_base[:], off_ps[:, 0:2], 1.0, None, ALU.add).then_inc(S["hist_step"], 1)
            d.wait_ge(S["hist_step"], 5)
            for c in range(2):
                m = v.tensor_scalar(base[:, c, :], upto[:, c, :], row_base[:, c:c + 1], None, ALU.add)
            m.then_inc(S["base_made"], 1)

            def look(bank, slot, hh, j, t):
                d.wait_ge(S["looked_up"], t + 1 + UNITS[0])
                d.wait_ge(S["look_free"], t - 2 + len(look_ps) + 1)
                v.scalar_tensor_tensor(out=junk_look[:, slot, :], in0=iota_f[:], scalar=dig[:, hh, 1, j:j + 1],
                                       in1=look_ps[bank][:, 0:DIGIT], op0=ALU.is_equal, op1=ALU.mult,
                                       accum_out=looked[:, hh % 2, j:j + 1]).then_inc(S["look_free"], 1)

            def places(c, hh):
                h = hh % 2
                d.wait_ge(S["look_free"], (c + 1) * CHUNK + len(look_ps))
                v.tensor_tensor(place[:], looked[:, h, :], same[:, h, :], ALU.add).then_inc(S["place_summed"], 1)
                d.wait_ge(S["place_summed"], c + 1)
                v.tensor_copy(place_i[:, hh, :], place[:]).then_inc(S["places_made"], 1)

            def chunks(i, first=False):
                for hh in range(UNROLL):
                    c = UNROLL * i + hh
                    h = hh % 2
                    next_digits(c, hh)
                    d.wait_ge(chunk_keys[h], 16 * (2 * i + hh // 2 + 1))
                    at_least(d, S["high_t_far"], c)
                    v.tensor_single_scalar(hirow, keyrow[:, h, :], 8, ALU.arith_shift_right).then_inc(S["hirow_made"], 1)
                    d.wait_ge(chunk_recs[hh], 16 * i + 16)
                    v.tensor_copy(recs[:, hh, :, W_NODE], digits[:, 2, bass.ds(c * CHUNK, CHUNK)])
                    v.tensor_copy(recs[:, hh, :, W_SOURCE].bitcast(I32), dst_i[:, bass.ds(c * CHUNK, CHUNK)])
                    d.wait_ge(S["hirow_made"], c + 1)
                    d.wait_ge(S["dig_made"], N_CHUNKS + c + 1)
                    v.tensor_scalar(onehot_t[:, h, 1, :], hirow, iota_p[:, 1:2], None, ALU.is_equal).then_inc(S["onehot_t_made"], 1)
                    for j in range(CHUNK):
                        k = hh * CHUNK + j
                        t = c * CHUNK + j
                        e = int(j >= UNITS[0])
                        r = j - e * UNITS[0]
                        if r == 0 and not (first and hh == 0):
                            d.wait_ge(S["counts_moved"], 2 * c + e)
                        onehots(hh, j, False)
                        d.wait_ge(S["same_made"], t + 1)
                        v.scalar_tensor_tensor(out=junk_same[:, k % 2, 0:(r + 1) * P], in0=keyrow[:, h, (j - r) * P:(j + 1) * P], scalar=dig[:, hh, 2, j:j + 1],
                                               in1=before[:, (UNITS[0] - 1 - r) * P:UNITS[0] * P], op0=ALU.is_equal, op1=ALU.mult,
                                               accum_out=same[:, h, j:j + 1]).then_inc(S["same_made"], 1)
                        if not (first and k < LAG):
                            kk = (k - LAG) % (UNROLL * CHUNK)
                            look(kk % 4, kk % 2, kk // CHUNK, kk % CHUNK, t - LAG)
                        if r == 0:
                            d.wait_ge(S["counts_upper"], 2 * c + e + 1)
                            v.tensor_tensor(counts_sb[:, e, 1, :, :], counts_ps[:].rearrange("p (a b) -> p a b", a=2),
                                            counts_sb[:, e, 0, :, :], ALU.subtract).then_inc(S["counts_split"], 1)
                        if j == LAG - 1 and not (first and hh == 0):
                            places(c - 1, (hh - 1) % UNROLL)

            chunks(0, first=True)
            with d.Fori(1, SORT_LOOPS) as i:
                chunks(i)
            for k in range(UNROLL * CHUNK - LAG, UNROLL * CHUNK):
                look(k % 4, k % 2, k // CHUNK, k % CHUNK, RANK_TILES - UNROLL * CHUNK + k)
            places(N_CHUNKS - 1, UNROLL - 1)

            def add_scalars(b, slot):
                d.wait_ge(S["s2_ready"], b + 1)
                v.tensor_tensor(xs[:, slot, :, 0:C], b_s[:].rearrange("p (g c) -> p g c", g=GROUP), xs[:, slot, :, 0:C], ALU.add).then_inc(S["s_added"], 1)

            def step(s, i, k):
                b, f, p = s, s + 1, s + 2
                known = isinstance(s, int)
                back, front, pre = (not known or s >= 0), (not known or 0 <= s + 1 < N_GROUPS), (not known or 0 <= s + 2 < N_GROUPS)
                early = not known or s + 3 < N_GROUPS
                fp, bp = (k + 1) % 2, k % 2
                q, z = (k + 1) % SLOTS, (k + 2) % SLOTS
                hv = [xg[:, z, j, C:D].rearrange("p (c i) -> p i c", i=3) for j in range(GROUP)]

                def combine(j):
                    d.wait_ge(S["z_ready"], 4 * b + j + 1)
                    d.wait_ge(S["sq_copied"], 4 * b + j + 1)
                    for c in range(3):
                        m = v.scalar_tensor_tensor(out=y[:, bp, j, (c + 1) * C:(c + 2) * C], in0=zq[:, j % 2, :], scalar=unit[:, k, j, c:c + 1],
                                                   in1=b_z[:, c * C:(c + 1) * C], op0=ALU.mult, op1=ALU.add)
                    m.then_inc(S["y_made"], 1)

                def add_vectors(j):
                    if j == 0:
                        d.wait_ge(xs_in[k], loads(i, k, 0, GROUP))
                    d.wait_ge(S["s_copied"], 4 * b + j + 1)
                    xv = xs[:, k, j, C:D].rearrange("p (c i) -> p i c", i=3)
                    v.tensor_tensor(xv, b_seg[:, C:D].rearrange("p (i c) -> p i c", i=3), xv, ALU.add).then_inc(S["v_added"], 1)

                def product(n, bank, w):
                    v.tensor_tensor(prod[:, fp, n, :], FB[bank][:], w_sb[:, w, :], ALU.mult).then_inc(S["prod_done"], 1)

                def projected(c):
                    for j in range(GROUP):
                        if c == 2:
                            d.wait_ge(S["g_part"], 4 * p + j + 1)
                        v.scalar_tensor_tensor(out=gsum[:, bp, c, j, :], in0=hv[j][:, c, :], scalar=unit[:, z, j, c:c + 1],
                                               in1=gsum[:, bp, c - 1, j, :], op0=ALU.mult, op1=ALU.add).then_inc(S["pre_made"] if c == 2 else S["g_part"], 1)

                def statistics(slot, j):
                    v.bn_stats(stats[:, j, :], xg[:, slot, j, :]).then_inc(S["stats_made"], 1)

                def next_product(n, bank, w):
                    d.wait_ge(S["j_ready"], 5 * f + (1, 1, 2, 3, 4, 5)[n])
                    if n < 4:
                        d.wait_ge(S["w_copied"], 4 * f + n + 1)
                    product(n, bank, w)

                def selection(tiles):
                    for j in tiles:
                        v.tensor_scalar(sel[:, fp, j, :], FB[0][:, j * P:(j + 1) * P], rec[:, q, j, W_NODE:W_NODE + 1],
                                        scale[:, fp, j:j + 1], ALU.is_equal, ALU.mult).then_inc(S["sel_made"], 1)

                def normalise(tiles):
                    for j in tiles:
                        v.tensor_scalar(xg[:, z, j, :], xg[:, z, j, :], mv[:, j, 0:1], 0.0, ALU.subtract, ALU.max).then_inc(S["h_made"], 1)

                if not known or s >= 1:
                    add_scalars(b - 1, (k - 1) % SLOTS)
                if front:
                    d.wait_ge(S["keyb_ready"], f + 1)
                    d.wait_ge(S["scale_made"], 2 * f + 2)
                    at_least(d, S["seg_ready"], 4 * (f - 1))
                    selection((0, 1))
                if back:
                    combine(0)
                if front:
                    selection((2, 3))
                if pre:
                    statistics(z, 2)
                if front:
                    d.wait_ge(S["sel_made"], 4 * f + 4)
                    v.tensor_copy(sel[:, fp, :, 0:1], sel[:, fp, :, P - 1:P]).then_inc(S["sel_done"], 1)
                if back:
                    combine(1)
                if pre:
                    statistics(z, 3)
                if back:
                    add_vectors(0)
                if pre:
                    at_least(d, S["h_made"], 4 * p)
                    at_least(d, S["var_made"], p)
                    wait_apart(d, S["stats_made"], 4 * p + 4, S["dve_passed"])
                    for j in range(GROUP):
                        v.bn_aggr(mv[:, j, :], stats[:, j, :]).then_inc(S["mv_made"], 1)
                    d.wait_ge(S["mv_made"], 4 * p + 4)
                    d.wait_ge(S["newton"], 4 * (s + 3))
                    v.tensor_scalar(var[:, 0:4], mv[:, :, 1], EPS, None, ALU.add).then_inc(S["var_made"], 1)
                if front:
                    d.wait_ge(S["f_ln"], f + 1)
                    at_least(d, S["w_ready"], 4 * f)
                    v.scalar_tensor_tensor(out=sp_t[:], in0=fr[:], scalar=-LOG2, in1=fa[:, 2, :], op0=ALU.add, op1=ALU.add).then_inc(S["sp_done"], 1)
                if pre:
                    normalise((0, 1))
                if back:
                    combine(2)
                    add_vectors(1)
                if pre:
                    normalise((2, 3))
                    d.wait_ge(S["unit_made"], p + 1)
                    at_least(d, S["t_ready"], 5 * (p - 1))
                    d.wait_ge(S["h_made"], 4 * p + 4)
                    v.tensor_tensor(gsum[:, bp, 0, :, :], xg[:, z, :, C:D].rearrange("p g (c i) -> p g i c", i=3)[:, :, 0, :],
                                    unit[:, z, :, 0:1].to_broadcast([P, GROUP, C]), ALU.mult).then_inc(S["g_first"], 1)
                if back:
                    combine(3)
                    add_vectors(2)
                if pre:
                    d.wait_ge(S["g_first"], p + 1)
                    projected(1)
                if front:
                    at_least(d, S["z_ready"], 4 * (f - 1))
                    next_product(0, 2, 0)
                    next_product(1, 2, 1)
                    next_product(2, 0, 2)
                if back:
                    add_vectors(3)
                if pre:
                    projected(2)
                if early:
                    d.wait_ge(xg_in[(k + 3) % SLOTS], loads(i, k, 3, GROUP))
                    at_least(d, S["mv_made"], 4 * (p + 1))
                    statistics((k + 3) % SLOTS, 0)
                if front:
                    next_product(3, 2, 3)
                if early:
                    statistics((k + 3) % SLOTS, 1)
                if back:
                    d.wait_ge(S["b_ln"], b + 1)
                    at_least(d, S["s2_ready"], b)
                    v.scalar_tensor_tensor(out=ssp_t[:], in0=br[:], scalar=-LOG2, in1=ba[:, 2, :], op0=ALU.add, op1=ALU.add).then_inc(S["ssp_done"], 1)
                if front:
                    next_product(4, 3, 3)
                    next_product(5, 0, 3)

            steps(d, step, -3)
            add_scalars(N_GROUPS - 1, (N_GROUPS - 1) % SLOTS)


_OUTS = [((N_NODES, D), "float32")]


def kernel(**inputs):
    import numpy as _np
    import concourse.bacc as _bacc
    from concourse import mybir as _mybir
    from concourse.bass_utils import run_bass_kernel_spmd as _run

    a = {k: _np.asarray(v) for k, v in inputs.items()}
    pad = RANK_TILES * P - N_EDGES
    src = _np.concatenate([a["src"].astype(_np.int32), _np.full(pad, PAD_KEY, _np.int32)]).reshape(P, RANK_TILES)
    dst = _np.concatenate([a["dst"].astype(_np.int32), _np.zeros(pad, _np.int32)]).reshape(P, RANK_TILES)
    attrs = _np.concatenate([a["edge_weight"][:, None], a["edge_attr_3"], a["edge_attr_20"]], axis=1)
    attrs = _np.concatenate([attrs, _np.ones((pad, ATTR), _np.float32)]).reshape(P, RANK_TILES * ATTR)
    given = {
        "x": a["x"], "src_cols": src, "src_rows": src.T.reshape(-1), "dst_cols": dst, "attrs": attrs,
        **{n: a["L0_gnn_" + n] for n in ("W_in2f_s", "W_in2f_v", "Wf1", "bf1", "Wf2", "bf2", "W1_s", "W1_v", "W2_s", "W2_v")},
    }
    nc = _bacc.Bacc("TRN2", target_bir_lowering=False, num_devices=1)
    arrays, args = {}, []
    for name, value in given.items():
        value = _np.ascontiguousarray(value)
        arrays[f"in_{name}_dram"] = value
        args.append(nc.dram_tensor(f"in_{name}_dram", value.shape, _mybir.dt.from_np(value.dtype), kind="ExternalInput").ap())
    for i, (shape, dtype) in enumerate(_OUTS):
        dt = _mybir.dt.from_np(_np.dtype(dtype))
        args.append(nc.dram_tensor(f"out_{i}_dram", shape, dt, kind="ExternalOutput").ap())
    gnn_kernel(nc, *args)
    r = _run(nc, [arrays], core_ids=[0])
    return r.results[0]["out_0_dram"]
```

```python
import math
from contextlib import ExitStack

import concourse.bass as bass
from concourse import mybir

F32 = mybir.dt.float32
I32 = mybir.dt.int32
BF16 = mybir.dt.bfloat16
ALU = mybir.AluOpType
ACT = mybir.ActivationFunctionType

P = 128
N_NODES = 50000
N_EDGES = 25000
D = 512
C = 128
N_RBF = 20
EPS = 1e-5
LOG2 = math.log(2.0)
Y0 = 1.0 / math.sqrt(4.0 * math.pi)
Y1_SCALE = math.sqrt(3.0 / (4.0 * math.pi))

RANK_TILES = -(-N_EDGES // P)
CHUNK = 7
N_CHUNKS = RANK_TILES // CHUNK
UNROLL = 4
UNITS = (4, 3)
LAG = 4
DIGIT = 256
HIGHS = N_NODES // DIGIT + 1
ACT_HIGHS = (1, 3, 5)
HIGH_SLOTS = 3
PAD_KEY = HIGHS * DIGIT - 1
ATTR = 4 + N_RBF
REC = 32
W_NODE, W_SOURCE, W_WEIGHT, W_VEC, W_RBF = 0, 1, 2, 3, 6

GROUP = 4
REAL = P - 1
N_GROUPS = -(-N_EDGES // (GROUP * REAL))
SORTED = RANK_TILES * P
PAD_ROWS = 11
N_ROWS = 1 + SORTED + PAD_ROWS * P
X_PARTS = (0, 0, 0, 1, 1, 2)
W_PARTS = (0, 1, 2, 0, 1, 0)
K_RBF = len(X_PARTS) * N_RBF
SKIP = 65536.0
SLOTS = 4
assert RANK_TILES % CHUNK == 0 and N_CHUNKS % UNROLL == 0 and N_GROUPS % SLOTS == 2
assert N_ROWS > GROUP * REAL * (N_GROUPS + 2) + 1

COPY_CHUNKS = 100
COPY_FIRST = 29
COPY_BESIDE = (3, 2, 3, 2)


def at_least(eng, sem, value):
    if not (isinstance(value, int) and value <= 0):
        eng.wait_ge(sem, value)


def wait_apart(eng, sem, value, passed):
    eng.wait_ge(sem, value)
    eng.sem_inc(passed, 1)


def gnn_kernel(nc, x, src_cols, src_rows, dst_cols, attrs, w_in_s, w_in_v, wf1, bf1, wf2, bf2,
               w1_s, w1_v, w2_s, w2_v, out):
    table = nc.dram_tensor("records_by_node", [N_ROWS, REC], F32, kind="Internal").ap()

    ctx = ExitStack()
    with ctx:
        def sb(name, shape, dt=F32):
            return ctx.enter_context(nc.sbuf_tensor(name, shape, dt))

        def sem(name):
            return ctx.enter_context(nc.semaphore(name))

        ident = sb("ident", [P, P])
        ones_m = sb("ones_m", [P, P])
        after = sb("after", [P, P])
        before = sb("before", [P, UNITS[0] * P])
        iota_f = sb("iota_f", [P, DIGIT])
        iota_b = sb("iota_b", [P, DIGIT], BF16)
        zeros_b = sb("zeros_b", [P, DIGIT], BF16)

        prod_room = sb("prod_room", [P, 2 * 6 * GROUP * P])
        y_room = sb("y_room", [P, 2 * GROUP * D])
        h_room = sb("h_room", [P, 5 * GROUP * P])
        h_t = h_room[:].rearrange("p (n e) -> p n e", n=5)
        prod = prod_room[:].rearrange("p (s n e) -> p s n e", s=2, n=6)
        y = y_room[:].rearrange("p (s g d) -> p s g d", s=2, g=GROUP)

        def part(room, start, *dims, dt=F32):
            per = 2 if dt == BF16 else 1
            flat = room[:, start:start + math.prod(dims) // per]
            if dt != F32:
                flat = flat.bitcast(dt)
            if len(dims) == 1:
                return flat
            names = "abcd"[:len(dims)]
            return flat.rearrange(f"p ({' '.join(names)}) -> p {' '.join(names)}", **dict(zip(names, dims)))

        TILE_KEYS = CHUNK * P
        onehot_t = part(prod_room, 0, 2, CHUNK, 2, P, dt=BF16)
        keyrow = part(prod_room, 2 * TILE_KEYS, UNROLL, TILE_KEYS, dt=I32)
        junk_same = part(prod_room, (2 + UNROLL) * TILE_KEYS, 2, UNITS[0] * P, dt=BF16)
        assert (2 + UNROLL) * TILE_KEYS + UNITS[0] * P <= 2 * 6 * GROUP * P
        onehot = part(h_room, 0, CHUNK, 2, DIGIT, dt=BF16)
        count, upto, base = (part(y_room, n * 2 * DIGIT, 2, DIGIT) for n in range(3))
        counts_sb = part(y_room, 6 * DIGIT, 2, 2, 2, DIGIT, dt=BF16)
        junk_look = part(y_room, 10 * DIGIT, 2, DIGIT)
        assert 12 * DIGIT <= 2 * GROUP * D

        key_i = sb("key_i", [P, RANK_TILES], I32)
        dst_i = sb("dst_i", [P, RANK_TILES], I32)
        digit_i = sb("digit_i", [P, 2, RANK_TILES], I32)
        digits = sb("digits", [P, 4, RANK_TILES + CHUNK])
        dig = sb("dig", [P, UNROLL, 4, CHUNK])
        high_far = sb("high_far", [P, HIGH_SLOTS + 1, HIGHS], BF16)
        row_total = sb("row_total", [P, 2])
        row_base = sb("row_base", [P, 2])
        looked = sb("looked", [P, 2, CHUNK])
        same = sb("same", [P, 2, CHUNK])
        place = sb("place", [P, CHUNK])
        place_i = sb("place_i", [P, UNROLL, CHUNK], I32)
        recs = sb("recs", [P, UNROLL, CHUNK, REC])
        padrec = sb("padrec", [P, PAD_ROWS, REC])

        wraw = sb("wraw", [P, 8, C])
        wf2_raw = sb("wf2_raw", [P, 4 * C])
        w_t = sb("w_t", [P, 2, C])
        wf1_sb = sb("wf1_sb", [N_RBF, C])
        wf1_rest = sb("wf1_rest", [N_RBF, C])
        wf1_parts = sb("wf1_parts", [N_RBF, 3, C], BF16)
        wf1_b = sb("wf1_b", [K_RBF, C], BF16)
        ident_b = sb("ident_b", [P, P], BF16)
        rbf = sb("rbf", [P, 2, GROUP, len(X_PARTS), N_RBF], BF16)
        rbf_rest = sb("rbf_rest", [P, GROUP, N_RBF])
        bf1_sb = sb("bf1_sb", [P, 1])
        bf2_sb = sb("bf2_sb", [P, 4])
        wf2_sb = sb("wf2_sb", [P, 4, C])
        w_a, w_b, m_a, m_b, u_c, u_d, w2_sb = (
            sb(n, [P, C]) for n in ("w_a", "w_b", "m_a", "m_b", "u_c", "u_d", "w2_sb"))

        rec = sb("rec", [P, SLOTS, GROUP, REC + 1])
        scat_i = sb("scat_i", [P, SLOTS, GROUP], I32)
        xg = sb("xg", [P, SLOTS, GROUP, D])
        xs = sb("xs", [P, SLOTS, GROUP, D])
        stats = sb("stats", [P, GROUP, 6])
        mv = sb("mv", [P, GROUP, 2])
        sq = sb("sq", [P, GROUP, 3])
        sq_sum = sb("sq_sum", [P, GROUP])
        idx_f = sb("idx_f", [P, 3, GROUP])
        minus_mean = sb("minus_mean", [P, GROUP])
        var = sb("var", [P, 8])
        rsq = sb("rsq", [P, 2, 8])
        newt = sb("newt", [P, 4, 8])
        scale = sb("scale", [P, 2, GROUP])
        unit = sb("unit", [P, SLOTS, GROUP, 3])
        gsum = sb("gsum", [P, 2, 3, GROUP, C])
        sel = sb("sel", [P, 2, GROUP, P])
        ft_sb = sb("ft_sb", [K_RBF, GROUP * P], BF16)
        fa = sb("fa", [P, 3, GROUP * P])
        fr = sb("fr", [P, GROUP * P])
        sp_t = sb("sp_t", [P, GROUP * P])
        sp_m = sb("sp_m", [P, GROUP * P])
        w_sb = sb("w_sb", [P, 4, GROUP * P])
        zq = sb("zq", [P, 2, C])
        s_sb = sb("s_sb", [P, GROUP, C])
        ba = sb("ba", [P, 3, GROUP * P])
        br = sb("br", [P, GROUP * P])
        ssp_t = sb("ssp_t", [P, GROUP * P])

        psum = [ctx.enter_context(nc.psum_tensor(f"bank{i}", [P, 512], F32)) for i in range(8)]
        FB = psum[0:4]
        b_sq, b_z, b_seg, b_s = psum[4:8]
        ft_ps = FB[1][0:K_RBF, 0:GROUP * P // 2].bitcast(BF16)
        counts_ps, off_ps, look_ps = psum[0], psum[1], psum[2:6]
        high_t_ps = [bank[:].bitcast(BF16).rearrange("p (t q e) -> p t q e", t=UNITS[0], q=2) for bank in psum[6:8]]

        S = {}
        for n in """keys_in iotas consts digits_made dig_made onehots_free onehots_made counts_upper counts_split
                    totals_made offsets_made base_made counts_moved looked_up look_free high_far_made high_made high_t_ready high_t_copied
                    same_made hist_step place_summed places_made pads_made pads_out
                    weights_in filter_parts filter_in rbf_copied rbf_rests weights_t weights_tc weights_u weights_made copied
                    idx_made squares rsq_made newton scale_made unit_made
                    stats_made mv_made mean_made var_made h_made g_first g_part pre_made
                    keyb_ready ft_ready h1_ready t_ready j_ready w_ready sq_ready z_ready seg_ready st_ready s2_ready
                    ft_copied h1_read f_exp f_ln t_copied w_copied sq_copied s_copied st_read b_exp b_ln
                    sel_made sel_done sp_done prod_done y_made v_added ssp_done s_added zeroed pool_passed dve_passed carried carry_start f_abs b_abs ys_made""".split():
            S[n] = sem(n)
        chunk_keys = [sem(f"chunk_keys{h}") for h in range(UNROLL)]
        chunk_recs = [sem(f"chunk_recs{h}") for h in range(UNROLL)]
        chunk_out = [sem(f"chunk_out{h}") for h in range(UNROLL)]
        rec_in = [sem(f"rec_in{k}") for k in range(SLOTS)]
        xg_in = [sem(f"xg_in{k}") for k in range(SLOTS)]
        xs_in = [sem(f"xs_in{k}") for k in range(SLOTS)]
        rows_out = [sem(f"rows_out{k}") for k in range(SLOTS)]
        SORT_LOOPS = N_CHUNKS // UNROLL
        N_LOOPS = N_GROUPS // SLOTS

        def steps(eng, step, first):
            for s in range(first, SLOTS):
                step(s, s // SLOTS, s % SLOTS)
            with eng.Fori(1, N_LOOPS) as i:
                for k in range(SLOTS):
                    step(SLOTS * i + k, i, k)
            for s in range(SLOTS * N_LOOPS, N_GROUPS):
                step(s, N_LOOPS, s % SLOTS)

        def loads(i, k, ahead, per):
            return per * 16 * (i + (k + ahead) // SLOTS + 1)

        block = ctx.enter_context(nc.Block())

        @block.sync
        def _(sp):
            sp.dma_start(key_i[:], src_cols).then_inc(S["keys_in"], 16)
            sp.dma_start(dst_i[:], dst_cols).then_inc(S["keys_in"], 16)
            for n, w in enumerate((w_in_s, w_in_v, w1_s[0:2 * C:2, :], w1_s[1:2 * C:2, :],
                                   w1_v[0:2 * C:2, :], w1_v[1:2 * C:2, :], w2_s, w2_v)):
                sp.dma_start(wraw[:, n, :], w).then_inc(S["weights_in"], 16)
            sp.dma_start(wf2_raw[:], wf2[:, 0:4 * C]).then_inc(S["weights_in"], 16)
            sp.dma_start(wf1_sb[:], wf1).then_inc(S["weights_in"], 16)
            sp.dma_start(bf1_sb[:], bf1.rearrange("(c a) -> c a", a=1)).then_inc(S["weights_in"], 16)
            for v in range(2):
                sp.dma_start(bf2_sb[:, 2 * v:2 * v + 2],
                             bf2[2 * C * v:2 * C * (v + 1)].rearrange("(c a) -> c a", a=2)).then_inc(S["weights_in"], 16)
            rows = src_rows.rearrange("(a n) -> a n", a=1)
            attr = attrs.rearrange("p (t w) -> p t w", w=ATTR)
            sp.wait_ge(S["consts"], 2)

            def load_keys(c, h):
                sp.dma_start(keyrow[:, h, :], rows[:, bass.ds(c * TILE_KEYS, TILE_KEYS)].to_broadcast([P, TILE_KEYS])).then_inc(chunk_keys[h], 16)

            def load_recs(c, hh):
                sp.dma_start(recs[:, hh, :, 2:2 + ATTR], attr[:, bass.ds(c * CHUNK, CHUNK), :]).then_inc(chunk_recs[hh], 16)

            for hh in range(UNROLL):
                load_keys(hh, hh)
                load_recs(hh, hh)
            per = N_NODES // 5 // COPY_CHUNKS
            x5 = x.rearrange("(a b) c -> a (b c)", b=5)
            o5 = out.rearrange("(a b) c -> a (b c)", b=5)

            def copy(c):
                sp.dma_start(o5[bass.ds(c * per, per), :], x5[bass.ds(c * per, per), :]).then_inc(S["copied"], 16)

            for c in range(COPY_FIRST):
                copy(c)

            with sp.Fori(1, SORT_LOOPS) as i:
                for hh in range(UNROLL):
                    c = UNROLL * i + hh
                    sp.wait_ge(S["same_made"], (c - UNROLL + 1) * CHUNK + 2)
                    load_keys(c, hh)
                    sp.wait_ge(chunk_out[hh], i * (16 * CHUNK))
                    load_recs(c, hh)
                    for n in range(COPY_BESIDE[hh]):
                        copy(i * sum(COPY_BESIDE) + (COPY_FIRST - sum(COPY_BESIDE) + sum(COPY_BESIDE[:hh]) + n))
            sp.wait_ge(S["filter_parts"], 4)
            for n, w in enumerate(W_PARTS):
                sp.dma_start(wf1_b[n * N_RBF:(n + 1) * N_RBF, :], wf1_parts[:, w, :]).then_inc(S["filter_in"], 16)
            sp.wait_ge(S["pads_made"], 3)
            sp.dma_start(table[0:1, :], padrec[0:1, 0, :]).then_inc(S["pads_out"], 16)
            sp.dma_start(table[1 + SORTED:N_ROWS, :].rearrange("(p a) w -> p a w", a=PAD_ROWS), padrec[:]).then_inc(S["pads_out"], 16)
            sp.wait_ge(S["pads_out"], 32)
            for hh in range(UNROLL):
                sp.wait_ge(chunk_out[hh], 16 * CHUNK * SORT_LOOPS)

            def load_rec(g, slot):
                src = bass.AP(table.tensor, g * (GROUP * REAL * REC), [[REC, P], [REAL * REC, GROUP], [1, REC + 1]])
                sp.dma_start(rec[:, slot, :, :], src).then_inc(rec_in[slot], 16)

            for g in range(SLOTS):
                load_rec(g, g)
            c = COPY_FIRST + (SORT_LOOPS - 1) * sum(COPY_BESIDE)
            for g in range(3):
                sp.wait_ge(xg_in[g], 16 * GROUP)
                for n in range((COPY_CHUNKS - c) // (3 - g)):
                    copy(c + n)
                c += (COPY_CHUNKS - c) // (3 - g)
            assert c == COPY_CHUNKS
            with sp.Fori(0, N_LOOPS) as i:
                for k in range(SLOTS):
                    s = SLOTS * i + k
                    sp.wait_ge(S["sel_done"], s + 1)
                    sp.wait_ge(S["rbf_rests"], 2 * s + 2)
                    sp.wait_ge(S["scale_made"], 2 * s + 2)
                    load_rec(s + SLOTS, k)
            for k in range(SLOTS):
                sp.wait_ge(rows_out[k], 16 * GROUP * len(range(k, N_GROUPS, SLOTS)))
            for k in range(2):
                sp.wait_ge(rec_in[(N_GROUPS + k) % SLOTS], 16 * (N_LOOPS + 1))

        @block.gpsimd
        def _(g):
            pool = nc.gpsimd
            pool.iota(iota_f[:], [[1, DIGIT]], base=0, channel_multiplier=0, allow_small_or_imprecise_dtypes=True).then_inc(S["iotas"], 1)
            pool.memset(ones_m[:], 1.0).then_inc(S["consts"], 1)
            pool.memset(recs[:], 0.0).then_inc(S["consts"], 1)
            pool.memset(zeros_b[:], 0.0).then_inc(S["consts"], 1)
            g.wait_ge(S["consts"], 3)
            for m, sign, op in ((ident[:], 1, ALU.is_equal), (after[:], -1, ALU.is_gt), (before[:, (UNITS[0] - 1) * P:UNITS[0] * P], 1, ALU.is_gt)):
                pool.affine_select(out=m, in_=ones_m[:], compare_op=op, fill=0.0, base=0,
                                   pattern=[[-sign, P]], channel_multiplier=sign).then_inc(S["consts"], 1)
            pool.memset(before[:, 0:(UNITS[0] - 1) * P], 1.0).then_inc(S["consts"], 1)
            pool.memset(padrec[:], 1.0).then_inc(S["pads_made"], 1)
            g.wait_ge(S["pads_made"], 1)
            pool.memset(padrec[:, :, W_NODE], float(PAD_KEY)).then_inc(S["pads_made"], 1)
            pool.memset(padrec[:, :, W_SOURCE].bitcast(I32), 0).then_inc(S["pads_made"], 1)
            pool.memset(xs[:], 0.0).then_inc(S["zeroed"], 1)
            pool.memset(var[:], 1.0).then_inc(S["zeroed"], 1)
            pool.tensor_copy(ident_b[:], ident[:]).then_inc(S["zeroed"], 1)

            made = S["filter_parts"]
            g.wait_ge(S["weights_in"], 16 * 13)
            pool.tensor_scalar(wf1_parts[:, 0, :], wf1_sb[:], 1.0, None, ALU.mult).then_inc(made, 1)
            g.wait_ge(made, 1)
            pool.tensor_tensor(wf1_rest[:], wf1_sb[:], wf1_parts[:, 0, :], ALU.subtract).then_inc(made, 1)
            g.wait_ge(made, 2)
            pool.tensor_scalar(wf1_parts[:, 1, :], wf1_rest[:], 1.0, None, ALU.mult).then_inc(made, 1)
            g.wait_ge(made, 3)
            pool.tensor_tensor(wf1_parts[:, 2, :], wf1_rest[:], wf1_parts[:, 1, :], ALU.subtract).then_inc(made, 1)
            last_row = g.to_reg(N_ROWS - 1)
            last_node = g.to_reg(N_NODES - 1)
            with g.Fori(0, SORT_LOOPS) as i:
                for hh in range(UNROLL):
                    c = UNROLL * i + hh
                    g.wait_ge(S["places_made"], c + 1)
                    g.sem_inc(S["pool_passed"], 1)
                    for j in range(CHUNK):
                        pool.indirect_dma_start(table, bass.IndirectOffsetOnAxis(ap=place_i[:, hh, j:j + 1], axis=0),
                                                recs[:, hh, j, :], None, bounds_check=last_row, oob_is_err=False).then_inc(chunk_out[hh], 16)

            def rows(b, slot):
                g.wait_ge(S["s_added"], b + 1)
                g.wait_ge(S["copied"], 16 * COPY_CHUNKS)
                g.sem_inc(S["pool_passed"], 1)
                for j in range(GROUP):
                    pool.indirect_dma_start(out, bass.IndirectOffsetOnAxis(ap=scat_i[:, slot, j:j + 1], axis=0),
                                            xs[:, slot, j, :], None, bounds_check=last_node, oob_is_err=False).then_inc(rows_out[slot], 16)

            def step(s, i, k):
                q = (k + 3) % SLOTS
                n = s + 3
                if n < N_GROUPS + 1 if isinstance(n, int) else True:
                    g.wait_ge(rec_in[q], loads(i, k, 3, 1))
                    at_least(g, S["t_ready"], 5 * s)
                    g.sem_inc(S["pool_passed"], 1)
                    for j in range(GROUP):
                        pool.indirect_dma_start(xg[:, q, j, :], None, x,
                                                bass.IndirectOffsetOnAxis(ap=rec[:, q, j, W_SOURCE:W_SOURCE + 1].bitcast(I32), axis=0),
                                                bounds_check=last_node, oob_is_err=False).then_inc(xg_in[q], 16)
                    vec = rec[:, q, :, W_VEC:W_VEC + 3]
                    at_least(g, S["rsq_made"], 2 * n)
                    pool.tensor_tensor(sq[:], vec, vec, ALU.mult).then_inc(S["squares"], 1)
                    g.wait_ge(S["squares"], 3 * n + 1)
                    pool.tensor_tensor(sq_sum[:], sq[:, :, 0], sq[:, :, 1], ALU.add).then_inc(S["squares"], 1)
                    g.wait_ge(S["squares"], 3 * n + 2)
                    at_least(g, S["newton"], 4 * n)
                    pool.tensor_tensor(var[:, 4:8], sq_sum[:], sq[:, :, 2], ALU.add).then_inc(S["squares"], 1)
                if not isinstance(s, int) or s >= 1:
                    rows(s - 1, (k - 1) % SLOTS)
                p = s + 2
                if not isinstance(p, int) or 0 <= p < N_GROUPS:
                    z = (k + 2) % SLOTS
                    at_least(g, rows_out[z], loads(i, k, -2, GROUP))
                    at_least(g, S["idx_made"], 5 * p + 5)
                    g.sem_inc(S["pool_passed"], 1)
                    for j in range(GROUP):
                        pool.indirect_dma_start(xs[:, z, j, :], None, x,
                                                bass.IndirectOffsetOnAxis(ap=scat_i[:, z, j:j + 1], axis=0),
                                                bounds_check=last_node, oob_is_err=False).then_inc(xs_in[z], 16)
                if not isinstance(n, int) or n < N_GROUPS + 1:
                    at_least(g, rows_out[q], loads(i, k, -1, GROUP))
                    node, following = rec[:, q, :, W_NODE], rec[:, q, :, REC]
                    pool.tensor_tensor(idx_f[:, 0, :], following, node, ALU.subtract).then_inc(S["idx_made"], 1)
                    wait_apart(g, S["idx_made"], 5 * n + 1, S["pool_passed"])
                    pool.tensor_scalar(idx_f[:, 1, :], idx_f[:, 0, :], 1.0, -SKIP, ALU.min, ALU.mult).then_inc(S["idx_made"], 1)
                    g.wait_ge(S["idx_made"], 5 * n + 2)
                    pool.tensor_tensor(idx_f[:, 2, :], idx_f[:, 1, :], node, ALU.add).then_inc(S["idx_made"], 1)
                    wait_apart(g, S["idx_made"], 5 * n + 3, S["pool_passed"])
                    pool.tensor_scalar(scat_i[:, q, :], idx_f[:, 2, :], SKIP, None, ALU.add).then_inc(S["idx_made"], 1)
                    wait_apart(g, S["idx_made"], 5 * n + 4, S["pool_passed"])
                    pool.memset(scat_i[0:1, q, :], int(SKIP)).then_inc(S["idx_made"], 1)
                if not isinstance(p, int) or p < N_GROUPS:
                    g.wait_ge(S["rsq_made"], 2 * n + 2)
                    pool.tensor_tensor(newt[:, 0, :], rsq[:, 1, :], rsq[:, 1, :], ALU.mult).then_inc(S["newton"], 1)
                    g.wait_ge(S["newton"], 4 * n + 1)
                    pool.tensor_tensor(newt[:, 1, :], newt[:, 0, :], var[:], ALU.mult).then_inc(S["newton"], 1)
                    wait_apart(g, S["newton"], 4 * n + 2, S["pool_passed"])
                    pool.tensor_scalar(newt[:, 2, :], newt[:, 1, :], -0.5, 1.5, ALU.mult, ALU.add).then_inc(S["newton"], 1)
                    g.wait_ge(S["newton"], 4 * n + 3)
                    at_least(g, S["unit_made"], n)
                    pool.tensor_tensor(newt[:, 3, :], newt[:, 2, :], rsq[:, 1, :], ALU.mult).then_inc(S["newton"], 1)
                    g.wait_ge(S["newton"], 4 * n + 4)
                    at_least(g, S["y_made"], 4 * s)
                    pool.tensor_tensor(unit[:, q, :, :], rec[:, q, :, W_VEC:W_VEC + 3],
                                       newt[:, 3, 4:8].rearrange("p (g a) -> p g a", a=1).to_broadcast([P, GROUP, 3]),
                                       ALU.mult).then_inc(S["unit_made"], 1)
                    if not isinstance(p, int) or p >= 0:
                        z = (k + 2) % SLOTS
                        at_least(g, S["sel_done"], s + 1)
                        pool.tensor_tensor(scale[:, k % 2, :], newt[:, 3, 0:4], rec[:, z, :, W_WEIGHT], ALU.mult).then_inc(S["scale_made"], 1)
                        wait_apart(g, S["scale_made"], 2 * p + 1, S["pool_passed"])
                        pool.memset(scale[0:1, k % 2, :], 1.0).then_inc(S["scale_made"], 1)
            g.wait_ge(S["zeroed"], 3)
            steps(g, step, -3)
            rows(N_GROUPS - 1, (N_GROUPS - 1) % SLOTS)
            g.wait_ge(xg_in[N_GROUPS % SLOTS], 16 * GROUP * (N_LOOPS + 1))

        @block.scalar
        def _(a):
            act = nc.scalar.activation
            root = 1.0 / math.sqrt(C)
            mix = 1.0 / math.sqrt(2 * C)
            nc.scalar.preload_act_table_set("natural_log_exp_and_others")
            a.sem_inc(S["high_made"], HIGH_SLOTS)

            def highs(tiles, slots, hh, n, free=None):
                for m, (j, slot) in enumerate(zip(tiles, slots)):
                    a.wait_ge(S["high_made"], n + m + 1)
                    act(high_far[:, slot, :], iota_b[:, 0:HIGHS], ACT.Abs, bias=dig[:, hh, 3, j:j + 1]).then_inc(S["high_far_made"], 1)
                for m, (j, slot) in enumerate(zip(tiles, slots)):
                    if free is not None:
                        a.wait_ge(S["onehots_free"], free + j + 1)
                    a.wait_ge(S["high_far_made"], n + m + 1)
                    act(onehot[:, j, 0, 0:HIGHS], high_far[:, slot, :], ACT.Relu, scale=-1.0, bias=1.0).then_inc(S["high_made"], 1)

            with a.Fori(0, SORT_LOOPS) as i:
                for hh in range(UNROLL):
                    c = UNROLL * i + hh
                    a.wait_ge(S["dig_made"], c + 1)
                    highs(ACT_HIGHS, range(HIGH_SLOTS), hh, c * len(ACT_HIGHS), free=c * CHUNK)

            a.wait_ge(S["weights_in"], 16 * 13)
            a.wait_ge(S["weights_t"], 1)
            act(w_t[:], b_sq[:, 0:2 * C].rearrange("p (a c) -> p a c", a=2), ACT.Copy).then_inc(S["weights_tc"], 1)
            for n, (dst, src, factor) in enumerate((
                    (w_a, wraw[:, 0, :], root), (w_b, wraw[:, 1, :], root),
                    (m_a, wraw[:, 2, :], mix * Y0), (m_b, wraw[:, 3, :], mix * Y1_SCALE / math.sqrt(3.0)),
                    (w2_sb, wraw[:, 6, :], root))):
                act(dst[:], src, ACT.Copy, scale=factor).then_inc(S["weights_made"], 1)
            for v in range(2):
                for b in range(2):
                    cols = wf2_raw[:, 2 * C * v:2 * C * (v + 1)].rearrange("p (c a) -> p a c", a=2)[:, b, :]
                    act(wf2_sb[:, 2 * v + b, :], cols, ACT.Copy).then_inc(S["weights_made"], 1)
            a.wait_ge(S["weights_u"], 1)
            act(u_c[:], b_z[:, 0:C], ACT.Copy, scale=mix * root * Y1_SCALE).then_inc(S["weights_made"], 1)
            act(u_d[:], b_z[:, C:2 * C], ACT.Copy, scale=mix * root * Y0).then_inc(S["weights_made"], 1)

            def upper_counts(c, e):
                a.wait_ge(S["counts_moved"], 2 * c + e + 1)
                a.wait_ge(S["looked_up"], c * CHUNK + (UNITS[0] - UNITS[1] if e == 0 else UNITS[0]))
                act(counts_sb[:, e, 0, :, :], counts_ps[:].rearrange("p (a b) -> p a b", a=2), ACT.Copy).then_inc(S["counts_upper"], 1)

            def high_rows(c, h, e):
                a.wait_ge(S["high_t_ready"], 2 * c + e + 1)
                start = e * UNITS[0]
                act(onehot_t[:, h, start:start + UNITS[e], :, :], high_t_ps[e][:, 0:UNITS[e], :, :], ACT.Copy).then_inc(S["high_t_copied"], 1)

            a.sem_inc(S["high_t_copied"], 2)

            def chunks(i, first=False):
                for hh in range(UNROLL):
                    c = UNROLL * i + hh
                    h = hh % 2
                    n = N_CHUNKS * len(ACT_HIGHS) + c * CHUNK
                    a.wait_ge(S["dig_made"], N_CHUNKS + c + 1)
                    if not (first and hh == 0):
                        a.wait_ge(S["counts_moved"], 2 * c)
                    highs((0, 1), (0, 1), hh, n)
                    upper_counts(c, 0)
                    highs((2, 3), (2, 3), hh, n + 2)
                    high_rows(c, h, 0)
                    if not (first and hh == 0):
                        a.wait_ge(S["counts_moved"], 2 * c + 1)
                    highs((4, 5), (0, 1), hh, n + 4)
                    upper_counts(c, 1)
                    highs((6,), (2,), hh, n + 6)
                    high_rows(c, h, 1)

            chunks(0, first=True)
            with a.Fori(1, SORT_LOOPS) as i:
                chunks(i)

            def t_copy(f, i):
                a.wait_ge(S["t_ready"], 5 * f + i + 1)
                at_least(a, S["j_ready"], 5 * f)
                act(h_t[:, i, :], FB[(3 + i) % 4][:], ACT.Copy).then_inc(S["t_copied"], 1)

            def w_copy(f, i):
                bank, bias = ((0, 0), (1, 2), (3, 1), (1, 3))[i]
                a.wait_ge(S["w_ready"], 4 * f + i + 1)
                at_least(a, S["prod_done"], 6 * f)
                act(w_sb[:, i, :], FB[bank][:], ACT.Identity, bias=bf2_sb[:, bias:bias + 1]).then_inc(S["w_copied"], 1)

            def sq_copy(b, k, j):
                a.wait_ge(S["sq_ready"], 4 * b + j + 1)
                act(y[:, k % 2, j, 0:C], b_sq[:, 0:C], ACT.Copy).then_inc(S["ys_made"], 1)
                act(zq[:, j % 2, :], b_sq[:, C:2 * C], ACT.Copy).then_inc(S["sq_copied"], 1)

            def s_copy(b, j):
                a.wait_ge(S["seg_ready"], 4 * b + j + 1)
                at_least(a, S["st_ready"], b)
                act(s_sb[:, j, :], b_seg[:, 0:C], ACT.Copy).then_inc(S["s_copied"], 1)

            def carry(t, par, j):
                a.wait_ge(S["v_added"], t + 1)
                a.wait_ge(S["y_made"], t + 2)
                a.wait_ge(S["ys_made"], t + 2)
                act(y[0:1, par, j, :], b_seg[0:1, :], ACT.Copy).then_inc(S["carried"], 1)

            def normalise(p, z, tiles):
                a.wait_ge(S["mean_made"], p + 1)
                for j in tiles:
                    act(xg[:, z, j, :], xg[:, z, j, :], ACT.Relu, bias=minus_mean[:, j:j + 1]).then_inc(S["h_made"], 1)

            def part_again(p, par, part_no):
                at, times = X_PARTS.index(part_no), X_PARTS.count(part_no) - 1
                a.wait_ge(S["rbf_copied"], 4 * p + (1, 2)[part_no])
                act(rbf[:, par, :, at + 1:at + 1 + times, :], rbf[:, par, :, at:at + 1, :].to_broadcast([P, GROUP, times, N_RBF]),
                    ACT.Copy).then_inc(S["rbf_copied"], 1)

            def step(s, i, k):
                b, f, n = s, s + 1, s + 3
                prep, early = (not isinstance(s, int) or 0 <= s + 2 < N_GROUPS), (not isinstance(s, int) or s + 3 < N_GROUPS)
                z = (k + 2) % SLOTS
                known = isinstance(s, int)
                back, front, pre = (not known or s >= 0), (not known or 0 <= s + 1 < N_GROUPS), (not known or s + 2 < N_GROUPS)
                if front:
                    a.wait_ge(S["ft_ready"], f + 1)
                    at_least(a, S["h1_ready"], f)
                    act(ft_sb[:], ft_ps, ACT.Copy).then_inc(S["ft_copied"], 1)
                if front:
                    a.wait_ge(S["h1_ready"], f + 1)
                    at_least(a, S["f_exp"], f)
                    act(fa[:, 0, :], FB[2][:], ACT.Abs, bias=bf1_sb[:]).then_inc(S["f_abs"], 1)
                if back:
                    sq_copy(b, k, 0)
                if front:
                    at_least(a, S["sp_done"], f)
                    act(fr[:], FB[2][:], ACT.Relu, bias=bf1_sb[:]).then_inc(S["h1_read"], 1)
                    a.wait_ge(S["f_abs"], f + 1)
                    at_least(a, S["f_ln"], f)
                    act(fa[:, 1, :], fa[:, 0, :], ACT.Exp, scale=-1.0).then_inc(S["f_exp"], 1)
                if back:
                    sq_copy(b, k, 1)
                    carry(4 * b - 1, k % 2, 0)
                if front:
                    a.wait_ge(S["f_exp"], f + 1)
                    act(fa[:, 2, :], fa[:, 1, :], ACT.Ln, bias=1.0).then_inc(S["f_ln"], 1)
                    t_copy(f, 0)
                if back:
                    s_copy(b, 0)
                if prep:
                    a.wait_ge(rec_in[z], loads(i, k, 2, 1))
                    at_least(a, S["ft_ready"], s + 1)
                    act(rbf[:, k % 2, :, X_PARTS.index(0), :], rec[:, z, :, W_RBF:W_RBF + N_RBF], ACT.Copy).then_inc(S["rbf_copied"], 1)
                    normalise(s + 2, z, (2,))
                if back:
                    carry(4 * b, k % 2, 1)
                if front:
                    t_copy(f, 1)
                    t_copy(f, 2)
                if back:
                    sq_copy(b, k, 2)
                    s_copy(b, 1)
                if prep:
                    a.wait_ge(S["rbf_rests"], 2 * (s + 2) + 1)
                    act(rbf[:, k % 2, :, X_PARTS.index(1), :], rbf_rest[:], ACT.Copy).then_inc(S["rbf_copied"], 1)
                    normalise(s + 2, z, (3,))
                if back:
                    carry(4 * b + 1, k % 2, 2)
                if front:
                    t_copy(f, 3)
                    t_copy(f, 4)
                if front:
                    w_copy(f, 0)
                if back:
                    sq_copy(b, k, 3)
                if pre:
                    at_least(a, S["var_made"], s + 3)
                    a.wait_ge(S["squares"], 3 * n + 3)
                    at_least(a, S["rsq_made"], 2 * n)
                    act(rsq[:, 0, :], var[:], ACT.Ln).then_inc(S["rsq_made"], 1)
                if front:
                    w_copy(f, 1)
                if pre:
                    a.wait_ge(S["rsq_made"], 2 * n + 1)
                    at_least(a, S["newton"], 4 * n)
                    act(rsq[:, 1, :], rsq[:, 0, :], ACT.Exp, scale=-0.5).then_inc(S["rsq_made"], 1)
                if back:
                    s_copy(b, 2)
                    carry(4 * b + 2, k % 2, 3)
                if front:
                    w_copy(f, 2)
                if prep:
                    part_again(s + 2, k % 2, 0)
                    part_again(s + 2, k % 2, 1)
                if back:
                    s_copy(b, 3)
                    a.wait_ge(S["st_ready"], b + 1)
                    at_least(a, S["b_exp"], b)
                    act(ba[:, 0, :], b_s[:], ACT.Abs).then_inc(S["b_abs"], 1)
                    at_least(a, S["ssp_done"], b)
                    act(br[:], b_s[:], ACT.Relu).then_inc(S["st_read"], 1)
                if front:
                    w_copy(f, 3)
                if back:
                    a.wait_ge(S["b_abs"], b + 1)
                    at_least(a, S["b_ln"], b)
                    act(ba[:, 1, :], ba[:, 0, :], ACT.Exp, scale=-1.0).then_inc(S["b_exp"], 1)
                    a.wait_ge(S["b_exp"], b + 1)
                    act(ba[:, 2, :], ba[:, 1, :], ACT.Ln, bias=1.0).then_inc(S["b_ln"], 1)
                if early:
                    normalise(s + 3, (k + 3) % SLOTS, (0, 1))

            a.wait_ge(S["zeroed"], 2)
            a.wait_ge(S["carry_start"], 1)
            steps(a, step, -3)

        @block.tensor
        def _(pe):
            mm, tr = nc.tensor.matmul, nc.tensor.transpose
            def add_counts(slot):
                for c in range(2):
                    rows = min(HIGHS - P * c, P)
                    m = mm(counts_ps[0:rows, DIGIT * c:DIGIT * (c + 1)], onehot[:, slot, 0, P * c:P * c + rows], onehot[:, slot, 1, :],
                           start=False, stop=False, skip_group_check=True)
                return m

            pe.wait_ge(S["consts"], 7)
            pe.sem_inc(S["onehots_free"], CHUNK)
            pe.sem_inc(S["looked_up"], UNITS[0])
            mm(counts_ps[:, 0:DIGIT], zeros_b[:, 0:P], zeros_b[:], start=True, stop=False, skip_group_check=True)
            mm(counts_ps[:, DIGIT:2 * DIGIT], zeros_b[:, 0:P], zeros_b[:], start=False, stop=False, skip_group_check=True)
            with pe.Fori(0, N_CHUNKS) as i:
                for k in range(CHUNK):
                    pe.wait_ge(S["onehots_made"], i * CHUNK + k + 1)
                    if k in ACT_HIGHS:
                        pe.wait_ge(S["high_made"], i * len(ACT_HIGHS) + ACT_HIGHS.index(k) + HIGH_SLOTS + 1)
                    add_counts(k).then_inc(S["onehots_free"], 1)
            pe.wait_ge(S["weights_in"], 16 * 13)
            tr(b_sq[:, 0:C], wraw[:, 4, :], ident[:])
            tr(b_sq[:, C:2 * C], wraw[:, 5, :], ident[:]).then_inc(S["weights_t"], 1)
            pe.wait_ge(S["weights_tc"], 1)
            mm(b_z[:, 0:C], w_t[:, 0, :], wraw[:, 7, :], start=True, stop=True)
            mm(b_z[:, C:2 * C], w_t[:, 1, :], wraw[:, 7, :], start=True, stop=True).then_inc(S["weights_u"], 1)
            pe.wait_ge(S["zeroed"], 3)
            for bank in psum[6:8]:
                for c in range(2):
                    mm(bank[:, DIGIT * c:DIGIT * (c + 1)], zeros_b[:, 0:P], zeros_b[:], start=True, stop=True)
            pe.wait_ge(S["totals_made"], 1)
            mm(off_ps[:, 0:1], after[:], row_total[:, 0:1], start=True, stop=True)
            mm(off_ps[:, 1:2], after[:], row_total[:, 1:2], start=True, stop=False)
            mm(off_ps[:, 1:2], ones_m[:], row_total[:, 0:1], start=False, stop=True).then_inc(S["offsets_made"], 1)
            pe.wait_ge(S["base_made"], 1)
            mm(counts_ps[:], ident[:], base.rearrange("p a b -> p (a b)"), start=True, stop=False, skip_group_check=True).then_inc(S["counts_moved"], 1)
            with pe.Fori(0, SORT_LOOPS) as i:
                for hh in range(UNROLL):
                    for e, start in enumerate((0, UNITS[0])):
                        tiles = range(start, start + UNITS[e])
                        pe.wait_ge(S["high_t_copied"], 2 * (UNROLL * i + hh) + e + 1)
                        for j in tiles:
                            pe.wait_ge(S["high_made"], N_CHUNKS * len(ACT_HIGHS) + (UNROLL * i + hh) * CHUNK + j + HIGH_SLOTS + 1)
                            tr(high_t_ps[e][:, j - start, 0, :], onehot[:, j, 0, 0:P], ident_b[:])
                            m = tr(high_t_ps[e][0:HIGHS - P, j - start, 1, :], onehot[:, j, 0, P:HIGHS], ident_b[:])
                        m.then_inc(S["high_t_ready"], 1)
                        pe.wait_ge(S["counts_split"], 2 * (UNROLL * i + hh) + e + 1)
                        for j in tiles:
                            pe.wait_ge(S["onehots_made"], RANK_TILES + (UNROLL * i + hh) * CHUNK + j + 1)
                            m = add_counts(j)
                        m.then_inc(S["counts_moved"], 1)
                        pe.wait_ge(S["high_t_copied"], 2 * (UNROLL * i + hh) + e + 3)
                        for j in tiles:
                            k = hh * CHUNK + j
                            pe.wait_ge(S["look_free"], i * (UNROLL * CHUNK) + k + 1)
                            for c in range(2):
                                rows = min(HIGHS - P * c, P)
                                for bits in range(2):
                                    m = mm(look_ps[k % 4][:, 0:DIGIT], onehot_t[0:rows, hh % 2, j, c, :], counts_sb[0:rows, e, bits, c, :],
                                           start=(c == 0 and bits == 0), stop=(c == 1 and bits == 1))
                            m.then_inc(S["looked_up"], 1)

            tile = [slice(j * P, (j + 1) * P) for j in range(GROUP)]

            def scalars_out(b):
                pe.wait_ge(S["ssp_done"], b + 1)
                pe.wait_ge(S["st_read"], b + 1)
                for j in range(GROUP):
                    m = mm(b_s[:, tile[j]], ssp_t[:, tile[j]], w2_sb[:], start=True, stop=True)
                m.then_inc(S["s2_ready"], 1)

            def step(s, i, k):
                b, f = s, s + 1
                known = isinstance(s, int)
                back, front = (not known or s >= 0), (not known or 0 <= s + 1 < N_GROUPS)
                q = (k + 1) % SLOTS
                fp, bp = (k + 1) % 2, k % 2

                def t_item(n):
                    bank = FB[(3 + n) % 4]
                    for j in range(GROUP):
                        if n == 4:
                            src = gsum[:, fp, 2, j, :]
                        elif n == 0:
                            src = xg[:, q, j, 0:C]
                        else:
                            src = xg[:, q, j, C:D].rearrange("p (c i) -> p i c", i=3)[:, n - 1, :]
                        m = tr(bank[:, tile[j]], src, ident[:])
                    m.then_inc(S["t_ready"], 1)

                def w_item(n):
                    bank, col = ((0, 0), (1, 2), (3, 1), (1, 3))[n]
                    mm(FB[bank][:], wf2_sb[:, col, :], sp_t[:], start=True, stop=True).then_inc(S["w_ready"], 1)

                def j_item(bank, w, n):
                    mm(FB[bank][:], w[:], h_t[:, n, :], start=True, stop=True).then_inc(S["j_ready"], 1)

                def scalar_messages(j):
                    at_least(pe, S["sq_copied"], 4 * b + j)
                    mm(b_sq[:, 0:C], prod[:, bp, 0, tile[j]], m_a[:], start=True, stop=False)
                    mm(b_sq[:, 0:C], prod[:, bp, 2, tile[j]], m_b[:], start=False, stop=True)
                    mm(b_sq[:, C:2 * C], prod[:, bp, 1, tile[j]], u_c[:], start=True, stop=True).then_inc(S["sq_ready"], 1)

                def vector_messages(j):
                    at_least(pe, S["y_made"], 4 * b + j)
                    for c in range(3):
                        m = mm(b_z[:, c * C:(c + 1) * C], prod[:, bp, 3 + c, tile[j]], u_d[:], start=True, stop=True)
                    m.then_inc(S["z_ready"], 1)

                def segment(j):
                    pe.wait_ge(S["y_made"], 4 * b + j + 1)
                    pe.wait_ge(S["carried"], 4 * b + j + 1)
                    mm(b_seg[:], sel[:, bp, j, :], y[:, bp, j, :], start=True, stop=True).then_inc(S["seg_ready"], 1)

                if front:
                    pe.wait_ge(rec_in[q], loads(i, k, 1, 1))
                    at_least(pe, S["w_copied"], 4 * f)
                    pe.wait_ge(S["rbf_copied"], 4 * f + 4)
                    pe.wait_ge(S["rbf_rests"], 2 * f + 2)
                    for j in range(GROUP):
                        m = tr(ft_ps[:, tile[j]], rbf[:, fp, j, :, :].rearrange("p a b -> p (a b)"), ident_b[:])
                    m.then_inc(S["ft_ready"], 1)
                if not known or s >= 1:
                    scalars_out(b - 1)
                if front:
                    pe.wait_ge(S["ft_copied"], f + 1)
                    at_least(pe, S["prod_done"], 6 * f - 2)
                    mm(FB[2][:], wf1_b[:], ft_sb[:], start=True, stop=True).then_inc(S["h1_ready"], 1)
                    at_least(pe, S["prod_done"], 6 * f)
                    for j in range(GROUP):
                        m = tr(FB[0][:, tile[j]], rec[:, q, j, W_NODE:W_NODE + 1].to_broadcast([P, P]), ident[:])
                    m.then_inc(S["keyb_ready"], 1)
                if back:
                    pe.wait_ge(S["prod_done"], 6 * b + 6)
                    scalar_messages(0)
                    vector_messages(0)
                    scalar_messages(1)
                if front:
                    pe.wait_ge(S["pre_made"], 4 * f + 4)
                    t_item(0)
                if back:
                    vector_messages(1)
                    pe.wait_ge(S["sel_done"], b + 1)
                    segment(0)
                if front:
                    pe.wait_ge(S["sel_made"], 4 * f + 4)
                    t_item(1)
                    pe.wait_ge(S["ft_copied"], f + 1)
                    t_item(2)
                if back:
                    scalar_messages(2)
                    vector_messages(2)
                    segment(1)
                if front:
                    pe.wait_ge(S["h1_read"], f + 1)
                    t_item(3)
                    pe.wait_ge(S["t_copied"], 5 * f + 1)
                    t_item(4)
                    pe.wait_ge(S["sp_done"], f + 1)
                    pe.wait_ge(S["t_copied"], 5 * f + 2)
                    w_item(0)
                if back:
                    scalar_messages(3)
                    vector_messages(3)
                if front:
                    pe.wait_ge(S["t_copied"], 5 * f + 3)
                    w_item(1)
                if back:
                    segment(2)
                if front:
                    pe.wait_ge(S["t_copied"], 5 * f + 4)
                    j_item(2, w_a, 0)
                    pe.wait_ge(S["t_copied"], 5 * f + 5)
                    w_item(2)
                if back:
                    segment(3)
                if front:
                    pe.wait_ge(S["w_copied"], 4 * f + 1)
                    j_item(0, w_b, 4)
                if back:
                    pe.wait_ge(S["s_copied"], 4 * b + 4)
                    at_least(pe, S["s_added"], b)
                    for j in range(GROUP):
                        m = tr(b_s[:, tile[j]], s_sb[:, j, :], ident[:])
                    m.then_inc(S["st_ready"], 1)
                if front:
                    pe.wait_ge(S["w_copied"], 4 * f + 2)
                    w_item(3)
                    pe.wait_ge(S["prod_done"], 6 * f + 2)
                    j_item(2, w_b, 1)
                    pe.wait_ge(S["w_copied"], 4 * f + 3)
                    j_item(3, w_b, 2)
                    pe.wait_ge(S["prod_done"], 6 * f + 3)
                    j_item(0, w_b, 3)

            pe.wait_ge(S["weights_made"], 11)
            pe.wait_ge(S["filter_in"], 16 * len(W_PARTS))
            pe.wait_ge(S["zeroed"], 3)
            mm(b_seg[:, 0:DIGIT], zeros_b[:, 0:P], zeros_b[:], start=True, stop=True)
            mm(b_seg[:, DIGIT:2 * DIGIT], zeros_b[:, 0:P], zeros_b[:], start=True, stop=True).then_inc(S["carry_start"], 1)
            steps(pe, step, -1)
            scalars_out(N_GROUPS - 1)

        @block.vector
        def _(d):
            v = nc.vector
            d.sem_inc(S["look_free"], len(look_ps))
            d.sem_inc(S["same_made"], 2)
            d.wait_ge(S["keys_in"], 32)
            v.tensor_single_scalar(digit_i[:, 0, :], key_i[:], 8, ALU.arith_shift_right).then_inc(S["digits_made"], 1)
            v.tensor_single_scalar(digit_i[:, 1, :], key_i[:], DIGIT - 1, ALU.bitwise_and).then_inc(S["digits_made"], 1)
            d.wait_ge(S["iotas"], 1)
            v.tensor_copy(iota_b[:], iota_f[:]).then_inc(S["digits_made"], 1)
            v.tensor_copy(digits[:, 2, 0:RANK_TILES], key_i[:]).then_inc(S["digits_made"], 1)
            d.wait_ge(S["digits_made"], 4)
            v.tensor_copy(digits[:, 0:2, 0:RANK_TILES], digit_i[:]).then_inc(S["digits_made"], 1)
            d.wait_ge(S["digits_made"], 5)
            v.tensor_scalar(digits[:, 3, 0:RANK_TILES], digits[:, 0, 0:RANK_TILES], -1.0, None, ALU.mult).then_inc(S["digits_made"], 1)
            d.wait_ge(S["digits_made"], 6)
            v.tensor_copy(digits[:, :, RANK_TILES:RANK_TILES + CHUNK], digits[:, :, 0:CHUNK]).then_inc(S["digits_made"], 1)
            v.tensor_copy(dig[:, 0, :, :], digits[:, :, 0:CHUNK]).then_inc(S["dig_made"], 1)
            d.wait_ge(S["digits_made"], 7)

            def next_digits(c, hh):
                v.tensor_copy(dig[:, (hh + 1) % UNROLL, :, :], digits[:, :, bass.ds((c + 1) * CHUNK, CHUNK)]).then_inc(S["dig_made"], 1)

            def onehots(hh, j, high):
                if high:
                    v.tensor_scalar(onehot[:, j, 0, 0:HIGHS], iota_b[:, 0:HIGHS], dig[:, hh, 0, j:j + 1], None, ALU.is_equal)
                v.tensor_scalar(onehot[:, j, 1, :], iota_b[:], dig[:, hh, 1, j:j + 1], None, ALU.is_equal).then_inc(S["onehots_made"], 1)

            with d.Fori(0, SORT_LOOPS) as i:
                for hh in range(UNROLL):
                    c = UNROLL * i + hh
                    next_digits(c, hh)
                    d.wait_ge(S["dig_made"], c + 1)
                    for j in range(CHUNK):
                        d.wait_ge(S["onehots_free"], c * CHUNK + j + 1)
                        onehots(hh, j, j not in ACT_HIGHS)
            d.wait_ge(S["onehots_free"], RANK_TILES + CHUNK)
            v.tensor_copy(count.rearrange("p a b -> p (a b)"), counts_ps[:]).then_inc(S["hist_step"], 1)
            d.wait_ge(S["hist_step"], 1)
            d.wait_ge(S["consts"], 7)
            for c in range(2):
                v.tensor_tensor_scan(upto[:, c, :], before[:, 0:DIGIT], count[:, c, :], 0.0, ALU.mult, ALU.add).then_inc(S["hist_step"], 1)
            d.wait_ge(S["hist_step"], 3)
            v.tensor_copy(row_total[:], upto[:, :, DIGIT - 1]).then_inc(S["totals_made"], 1)
            d.wait_ge(S["totals_made"], 1)
            v.tensor_tensor(upto, upto, count, ALU.subtract).then_inc(S["hist_step"], 1)
            d.wait_ge(S["offsets_made"], 1)
            v.tensor_scalar(row_base[:], off_ps[:, 0:2], 1.0, None, ALU.add).then_inc(S["hist_step"], 1)
            d.wait_ge(S["hist_step"], 5)
            for c in range(2):
                m = v.tensor_scalar(base[:, c, :], upto[:, c, :], row_base[:, c:c + 1], None, ALU.add)
            m.then_inc(S["base_made"], 1)

            def look(bank, slot, hh, j, t):
                d.wait_ge(S["looked_up"], t + 1 + UNITS[0])
                d.wait_ge(S["look_free"], t - 2 + len(look_ps) + 1)
                v.scalar_tensor_tensor(out=junk_look[:, slot, :], in0=iota_f[:], scalar=dig[:, hh, 1, j:j + 1],
                                       in1=look_ps[bank][:, 0:DIGIT], op0=ALU.is_equal, op1=ALU.mult,
                                       accum_out=looked[:, hh % 2, j:j + 1]).then_inc(S["look_free"], 1)

            def places(c, hh):
                h = hh % 2
                d.wait_ge(S["look_free"], (c + 1) * CHUNK + len(look_ps))
                v.tensor_tensor(place[:], looked[:, h, :], same[:, h, :], ALU.add).then_inc(S["place_summed"], 1)
                d.wait_ge(S["place_summed"], c + 1)
                v.tensor_copy(place_i[:, hh, :], place[:]).then_inc(S["places_made"], 1)

            def chunks(i, first=False):
                for hh in range(UNROLL):
                    c = UNROLL * i + hh
                    h = hh % 2
                    next_digits(c, hh)
                    d.wait_ge(chunk_keys[hh], 16 * i + 16)
                    d.wait_ge(chunk_recs[hh], 16 * i + 16)
                    v.tensor_copy(recs[:, hh, :, W_NODE], digits[:, 2, bass.ds(c * CHUNK, CHUNK)])
                    v.tensor_copy(recs[:, hh, :, W_SOURCE].bitcast(I32), dst_i[:, bass.ds(c * CHUNK, CHUNK)])
                    d.wait_ge(S["dig_made"], N_CHUNKS + c + 1)
                    for j in range(CHUNK):
                        k = hh * CHUNK + j
                        t = c * CHUNK + j
                        e = int(j >= UNITS[0])
                        r = j - e * UNITS[0]
                        if r == 0 and not (first and hh == 0):
                            d.wait_ge(S["counts_moved"], 2 * c + e)
                        onehots(hh, j, False)
                        d.wait_ge(S["same_made"], t + 1)
                        v.scalar_tensor_tensor(out=junk_same[:, k % 2, 0:(r + 1) * P], in0=keyrow[:, hh, (j - r) * P:(j + 1) * P], scalar=dig[:, hh, 2, j:j + 1],
                                               in1=before[:, (UNITS[0] - 1 - r) * P:UNITS[0] * P], op0=ALU.is_equal, op1=ALU.mult,
                                               accum_out=same[:, h, j:j + 1]).then_inc(S["same_made"], 1)
                        if not (first and k < LAG):
                            kk = (k - LAG) % (UNROLL * CHUNK)
                            look(kk % 4, kk % 2, kk // CHUNK, kk % CHUNK, t - LAG)
                        if r == 0:
                            d.wait_ge(S["counts_upper"], 2 * c + e + 1)
                            v.tensor_tensor(counts_sb[:, e, 1, :, :], counts_ps[:].rearrange("p (a b) -> p a b", a=2),
                                            counts_sb[:, e, 0, :, :], ALU.subtract).then_inc(S["counts_split"], 1)
                        if j == LAG - 1 and not (first and hh == 0):
                            places(c - 1, (hh - 1) % UNROLL)

            chunks(0, first=True)
            with d.Fori(1, SORT_LOOPS) as i:
                chunks(i)
            for k in range(UNROLL * CHUNK - LAG, UNROLL * CHUNK):
                look(k % 4, k % 2, k // CHUNK, k % CHUNK, RANK_TILES - UNROLL * CHUNK + k)
            places(N_CHUNKS - 1, UNROLL - 1)

            def add_scalars(b, slot):
                d.wait_ge(S["s2_ready"], b + 1)
                v.tensor_tensor(xs[:, slot, :, 0:C], b_s[:].rearrange("p (g c) -> p g c", g=GROUP), xs[:, slot, :, 0:C], ALU.add).then_inc(S["s_added"], 1)

            def step(s, i, k):
                b, f, p = s, s + 1, s + 2
                known = isinstance(s, int)
                back, front, pre = (not known or s >= 0), (not known or 0 <= s + 1 < N_GROUPS), (not known or 0 <= s + 2 < N_GROUPS)
                early = not known or s + 3 < N_GROUPS
                fp, bp = (k + 1) % 2, k % 2
                q, z = (k + 1) % SLOTS, (k + 2) % SLOTS
                hv = [xg[:, z, j, C:D].rearrange("p (c i) -> p i c", i=3) for j in range(GROUP)]

                def combine(j):
                    d.wait_ge(S["z_ready"], 4 * b + j + 1)
                    d.wait_ge(S["sq_copied"], 4 * b + j + 1)
                    for c in range(3):
                        m = v.scalar_tensor_tensor(out=y[:, bp, j, (c + 1) * C:(c + 2) * C], in0=zq[:, j % 2, :], scalar=unit[:, k, j, c:c + 1],
                                                   in1=b_z[:, c * C:(c + 1) * C], op0=ALU.mult, op1=ALU.add)
                    m.then_inc(S["y_made"], 1)

                def add_vectors(j):
                    if j == 0:
                        d.wait_ge(xs_in[k], loads(i, k, 0, GROUP))
                    d.wait_ge(S["s_copied"], 4 * b + j + 1)
                    xv = xs[:, k, j, C:D].rearrange("p (c i) -> p i c", i=3)
                    v.tensor_tensor(xv, b_seg[:, C:D].rearrange("p (i c) -> p i c", i=3), xv, ALU.add).then_inc(S["v_added"], 1)

                def product(n, bank, w):
                    v.tensor_tensor(prod[:, fp, n, :], FB[bank][:], w_sb[:, w, :], ALU.mult).then_inc(S["prod_done"], 1)

                def projected(c):
                    for j in range(GROUP):
                        if c == 2:
                            d.wait_ge(S["g_part"], 4 * p + j + 1)
                        v.scalar_tensor_tensor(out=gsum[:, bp, c, j, :], in0=hv[j][:, c, :], scalar=unit[:, z, j, c:c + 1],
                                               in1=gsum[:, bp, c - 1, j, :], op0=ALU.mult, op1=ALU.add).then_inc(S["pre_made"] if c == 2 else S["g_part"], 1)

                def statistics(tiles):
                    for j in tiles:
                        v.bn_stats(stats[:, j, :], xg[:, (k + 3) % SLOTS, j, :]).then_inc(S["stats_made"], 1)

                def next_product(n, bank, w):
                    d.wait_ge(S["j_ready"], 5 * f + (1, 1, 2, 3, 4, 5)[n])
                    if n < 4:
                        d.wait_ge(S["w_copied"], 4 * f + n + 1)
                    product(n, bank, w)

                def selection(tiles):
                    for j in tiles:
                        v.tensor_scalar(sel[:, fp, j, :], FB[0][:, j * P:(j + 1) * P], rec[:, q, j, W_NODE:W_NODE + 1],
                                        scale[:, fp, j:j + 1], ALU.is_equal, ALU.mult).then_inc(S["sel_made"], 1)

                if not known or s >= 1:
                    add_scalars(b - 1, (k - 1) % SLOTS)
                if front:
                    d.wait_ge(S["keyb_ready"], f + 1)
                    d.wait_ge(S["scale_made"], 2 * f + 2)
                    at_least(d, S["seg_ready"], 4 * (f - 1))
                    selection((0, 1, 2))
                if back:
                    combine(0)
                if front:
                    selection((3,))
                    d.wait_ge(S["sel_made"], 4 * f + 4)
                    v.tensor_copy(sel[:, fp, :, 0:1], sel[:, fp, :, P - 1:P]).then_inc(S["sel_done"], 1)
                if pre:
                    d.wait_ge(S["mv_made"], 4 * p + 4)
                    d.wait_ge(S["newton"], 4 * (s + 3))
                    v.tensor_scalar(var[:, 0:4], mv[:, :, 1], EPS, None, ALU.add).then_inc(S["var_made"], 1)
                if back:
                    combine(1)
                    add_vectors(0)
                if front:
                    d.wait_ge(S["f_ln"], f + 1)
                    at_least(d, S["w_ready"], 4 * f)
                    v.scalar_tensor_tensor(out=sp_t[:], in0=fr[:], scalar=-LOG2, in1=fa[:, 2, :], op0=ALU.add, op1=ALU.add).then_inc(S["sp_done"], 1)
                if pre:
                    d.wait_ge(S["rbf_copied"], 4 * p + 1)
                    v.tensor_tensor(rbf_rest[:], rec[:, z, :, W_RBF:W_RBF + N_RBF], rbf[:, bp, :, X_PARTS.index(0), :], ALU.subtract).then_inc(S["rbf_rests"], 1)
                if early:
                    d.wait_ge(xg_in[(k + 3) % SLOTS], loads(i, k, 3, GROUP))
                    at_least(d, S["mv_made"], 4 * (p + 1))
                    statistics((0, 1))
                if back:
                    combine(2)
                    add_vectors(1)
                if early:
                    statistics((2, 3))
                if pre:
                    d.wait_ge(S["unit_made"], p + 1)
                    at_least(d, S["t_ready"], 5 * (p - 1))
                    d.wait_ge(S["h_made"], 4 * p + 4)
                    v.tensor_tensor(gsum[:, bp, 0, :, :], xg[:, z, :, C:D].rearrange("p g (c i) -> p g i c", i=3)[:, :, 0, :],
                                    unit[:, z, :, 0:1].to_broadcast([P, GROUP, C]), ALU.mult).then_inc(S["g_first"], 1)
                    d.wait_ge(S["rbf_copied"], 4 * p + 2)
                    v.tensor_tensor(rbf[:, bp, :, X_PARTS.index(2), :], rbf_rest[:], rbf[:, bp, :, X_PARTS.index(1), :], ALU.subtract).then_inc(S["rbf_rests"], 1)
                if back:
                    combine(3)
                if early:
                    at_least(d, S["var_made"], p + 1)
                    wait_apart(d, S["stats_made"], 4 * (p + 1) + 4, S["dve_passed"])
                    for j in range(GROUP):
                        v.bn_aggr(mv[:, j, :], stats[:, j, :]).then_inc(S["mv_made"], 1)
                if back:
                    add_vectors(2)
                if pre:
                    d.wait_ge(S["g_first"], p + 1)
                    projected(1)
                if early:
                    at_least(d, S["h_made"], 4 * (p + 1))
                    d.wait_ge(S["mv_made"], 4 * (p + 1) + 4)
                    v.tensor_scalar(minus_mean[:], mv[:, :, 0], -1.0, None, ALU.mult).then_inc(S["mean_made"], 1)
                if front:
                    at_least(d, S["z_ready"], 4 * (f - 1))
                    next_product(0, 2, 0)
                    next_product(1, 2, 1)
                    next_product(2, 0, 2)
                if back:
                    add_vectors(3)
                if pre:
                    projected(2)
                if front:
                    next_product(3, 2, 3)
                if back:
                    d.wait_ge(S["b_ln"], b + 1)
                    at_least(d, S["s2_ready"], b)
                    v.scalar_tensor_tensor(out=ssp_t[:], in0=br[:], scalar=-LOG2, in1=ba[:, 2, :], op0=ALU.add, op1=ALU.add).then_inc(S["ssp_done"], 1)
                if front:
                    next_product(4, 3, 3)
                    next_product(5, 0, 3)

            steps(d, step, -3)
            add_scalars(N_GROUPS - 1, (N_GROUPS - 1) % SLOTS)


_OUTS = [((N_NODES, D), "float32")]


def kernel(**inputs):
    import numpy as _np
    import concourse.bacc as _bacc
    from concourse import mybir as _mybir
    from concourse.bass_utils import run_bass_kernel_spmd as _run

    a = {k: _np.asarray(v) for k, v in inputs.items()}
    pad = RANK_TILES * P - N_EDGES
    src = _np.concatenate([a["src"].astype(_np.int32), _np.full(pad, PAD_KEY, _np.int32)]).reshape(P, RANK_TILES)
    dst = _np.concatenate([a["dst"].astype(_np.int32), _np.zeros(pad, _np.int32)]).reshape(P, RANK_TILES)
    attrs = _np.concatenate([a["edge_weight"][:, None], a["edge_attr_3"], a["edge_attr_20"]], axis=1)
    attrs = _np.concatenate([attrs, _np.ones((pad, ATTR), _np.float32)]).reshape(P, RANK_TILES * ATTR)
    given = {
        "x": a["x"], "src_cols": src, "src_rows": src.T.reshape(-1), "dst_cols": dst, "attrs": attrs,
        **{n: a["L0_gnn_" + n] for n in ("W_in2f_s", "W_in2f_v", "Wf1", "bf1", "Wf2", "bf2", "W1_s", "W1_v", "W2_s", "W2_v")},
    }
    nc = _bacc.Bacc("TRN2", target_bir_lowering=False, num_devices=1)
    arrays, args = {}, []
    for name, value in given.items():
        value = _np.ascontiguousarray(value)
        arrays[f"in_{name}_dram"] = value
        args.append(nc.dram_tensor(f"in_{name}_dram", value.shape, _mybir.dt.from_np(value.dtype), kind="ExternalInput").ap())
    for i, (shape, dtype) in enumerate(_OUTS):
        dt = _mybir.dt.from_np(_np.dtype(dtype))
        args.append(nc.dram_tensor(f"out_{i}_dram", shape, dt, kind="ExternalOutput").ap())
    gnn_kernel(nc, *args)
    r = _run(nc, [arrays], core_ids=[0])
    return r.results[0]["out_0_dram"]
```
